# Optimizing a Trainium2 kernel written in Bass

```python
import numpy as np
import jax
import jax.numpy as jnp

def _softmax(x, axis=-1):
    return jax.nn.softmax(x, axis=axis)

def _gelu(x):
    return jax.nn.gelu(x, approximate=True)

def _silu(x):
    return jax.nn.silu(x)

def _sigmoid(x):
    return jax.nn.sigmoid(x)

def _layernorm(x, axis=-1, eps=1e-05):
    m = jnp.mean(x, axis=axis, keepdims=True)
    v = jnp.var(x, axis=axis, keepdims=True)
    return (x - m) / jnp.sqrt(v + eps)

def _scatter_add(tgt, idx, src, axis=0):
    return tgt.at[idx].add(src)

def _segment_sum(src, seg, n):
    return jax.ops.segment_sum(src, seg, n)
kernel_name = 'mk_conv_attn_hybrid_d2_conv_nhwc768_r4_7e7bc7'

def setup_inputs(seed: int=0):
    np.random.seed(seed)
    _w = jnp.asarray

    def _rec_inputs():
        import jax
        import jax.numpy as jnp
        _gk = jax.random.key(seed)
        x = -0.0001538 + 1 * jax.random.normal(jax.random.fold_in(_gk, 1), (8, 32, 32, 192), jnp.float32)
        return x
    x = _rec_inputs()

    def _L0_conv_setup():
        import jax, jax.numpy as jnp
        import numpy as np
        NUM_HEADS = 12

        def _rel_pos_table(size, rel_pos):
            coords = jnp.arange(size)[:, None] - jnp.arange(size)[None, :] + (size - 1)
            return rel_pos[coords]
        key = jax.random.key(seed)
        ks = jax.random.split(key, 5)
        B, H, W, C = (8, 32, 32, 192)
        hd = C // NUM_HEADS
        x = jax.random.normal(ks[0], (B, H, W, C), dtype=jnp.float32)
        qkv_w = jax.random.normal(ks[1], (C, 3 * C), dtype=jnp.float32) * 0.02
        qkv_b = jnp.zeros((3 * C,), dtype=jnp.float32)
        proj_w = jax.random.normal(ks[2], (C, C), dtype=jnp.float32) * 0.02
        proj_b = jnp.zeros((C,), dtype=jnp.float32)
        rel_pos_h = jax.random.normal(ks[3], (2 * H - 1, hd), dtype=jnp.float32) * 0.02
        rel_pos_w = jax.random.normal(ks[4], (2 * W - 1, hd), dtype=jnp.float32) * 0.02
        return {'x': x, 'qkv_w': qkv_w, 'qkv_b': qkv_b, 'proj_w': proj_w, 'proj_b': proj_b, 'rel_pos_h': rel_pos_h, 'rel_pos_w': rel_pos_w}
    _L0_conv_all = _L0_conv_setup()
    _L0_conv_in = {k: v for k, v in _L0_conv_all.items() if k in ('qkv_w', 'qkv_b', 'proj_w', 'proj_b', 'rel_pos_h', 'rel_pos_w')}
    del _L0_conv_all

    def _L1_attn_setup():
        import jax, jax.numpy as jnp
        import numpy as np
        HIDDEN = 192
        HEADS = 12
        HEAD_DIM = HIDDEN // HEADS
        NORM = float(np.sqrt(HIDDEN))
        key = jax.random.key(seed)
        ks = jax.random.split(key, 7)
        B, S, H = (8, 256, HIDDEN)
        scale = 0.02
        return {'hidden_states': jax.random.normal(ks[0], (B, S, H), dtype=jnp.float32), 'Wq': jax.random.normal(ks[1], (H, H), dtype=jnp.float32) * scale, 'bq': jax.random.normal(ks[2], (H,), dtype=jnp.float32) * scale, 'Wk': jax.random.normal(ks[3], (H, H), dtype=jnp.float32) * scale, 'bk': jax.random.normal(ks[4], (H,), dtype=jnp.float32) * scale, 'Wv': jax.random.normal(ks[5], (H, H), dtype=jnp.float32) * scale, 'bv': jax.random.normal(ks[6], (H,), dtype=jnp.float32) * scale}
    _L1_attn_all = _L1_attn_setup()
    _L1_attn_in = {k: v for k, v in _L1_attn_all.items() if k in ('Wq', 'bq', 'Wk', 'bk', 'Wv', 'bv')}
    del _L1_attn_all

    def _L1_ffn_setup():
        import jax, jax.numpy as jnp
        import numpy as np
        E, D, H = (16, 192, 192)
        B, N = (32, 197)
        key = jax.random.key(seed)
        ks = jax.random.split(key, 7)
        s = 0.02
        return {'x': jax.random.normal(ks[0], (B, N, D), dtype=jnp.float32), 'W1': jax.random.normal(ks[1], (E, H, D), dtype=jnp.float32) * s, 'b1': jax.random.normal(ks[2], (E, H), dtype=jnp.float32) * s, 'W2': jax.random.normal(ks[3], (E, D, H), dtype=jnp.float32) * s, 'b2': jax.random.normal(ks[4], (E, D), dtype=jnp.float32) * s, 'Wg': jax.random.normal(ks[5], (E, D), dtype=jnp.float32) * s, 'bg': jnp.zeros((E,), dtype=jnp.float32)}
    _L1_ffn_all = _L1_ffn_setup()
    _L1_ffn_in = {k: v for k, v in _L1_ffn_all.items() if k in ('W1', 'b1', 'W2', 'b2', 'Wg', 'bg')}
    del _L1_ffn_all
    return {'x': x, 'L0_conv_qkv_w': _L0_conv_in['qkv_w'], 'L0_conv_qkv_b': _L0_conv_in['qkv_b'], 'L0_conv_proj_w': _L0_conv_in['proj_w'], 'L0_conv_proj_b': _L0_conv_in['proj_b'], 'L0_conv_rel_pos_h': _L0_conv_in['rel_pos_h'], 'L0_conv_rel_pos_w': _L0_conv_in['rel_pos_w'], 'L1_attn_Wq': _L1_attn_in['Wq'], 'L1_attn_bq': _L1_attn_in['bq'], 'L1_attn_Wk': _L1_attn_in['Wk'], 'L1_attn_bk': _L1_attn_in['bk'], 'L1_attn_Wv': _L1_attn_in['Wv'], 'L1_attn_bv': _L1_attn_in['bv'], 'L1_ffn_W1': _L1_ffn_in['W1'], 'L1_ffn_b1': _L1_ffn_in['b1'], 'L1_ffn_W2': _L1_ffn_in['W2'], 'L1_ffn_b2': _L1_ffn_in['b2'], 'L1_ffn_Wg': _L1_ffn_in['Wg'], 'L1_ffn_bg': _L1_ffn_in['bg']}

def reference(x, L0_conv_qkv_w, L0_conv_qkv_b, L0_conv_proj_w, L0_conv_proj_b, L0_conv_rel_pos_h, L0_conv_rel_pos_w, L1_attn_Wq, L1_attn_bq, L1_attn_Wk, L1_attn_bk, L1_attn_Wv, L1_attn_bv, L1_ffn_W1, L1_ffn_b1, L1_ffn_W2, L1_ffn_b2, L1_ffn_Wg, L1_ffn_bg):
    import jax
    import jax.numpy as jnp

    def _L0_conv_ref(x, qkv_w, qkv_b, proj_w, proj_b, rel_pos_h, rel_pos_w):
        import jax, jax.numpy as jnp
        import numpy as np
        NUM_HEADS = 12

        def _rel_pos_table(size, rel_pos):
            coords = jnp.arange(size)[:, None] - jnp.arange(size)[None, :] + (size - 1)
            return rel_pos[coords]
        B, H, W, C = x.shape
        nh = NUM_HEADS
        hd = C // nh
        scale = hd ** (-0.5)
        L = H * W
        qkv = x.reshape(B, L, C) @ qkv_w + qkv_b
        qkv = qkv.reshape(B, L, 3, nh, hd).transpose(2, 0, 3, 1, 4)
        q, k, v = (qkv[0], qkv[1], qkv[2])
        attn = jnp.einsum('bhqd,bhkd->bhqk', q * scale, k)
        Rh = _rel_pos_table(H, rel_pos_h)
        Rw = _rel_pos_table(W, rel_pos_w)
        rq = q.reshape(B, nh, H, W, hd)
        rel_h = jnp.einsum('bnhwd,hkd->bnhwk', rq, Rh)
        rel_w = jnp.einsum('bnhwd,wkd->bnhwk', rq, Rw)
        attn = (attn.reshape(B, nh, H, W, H, W) + rel_h[..., :, None] + rel_w[..., None, :]).reshape(B, nh, L, L)
        attn = jax.nn.softmax(attn, axis=-1)
        out = jnp.einsum('bhqk,bhkd->bhqd', attn, v)
        out = out.reshape(B, nh, H, W, hd).transpose(0, 2, 3, 1, 4).reshape(B, H, W, C)
        return out @ proj_w + proj_b

    def _L1_attn_ref(hidden_states, Wq, bq, Wk, bk, Wv, bv):
        import jax, jax.numpy as jnp
        import numpy as np
        HIDDEN = 192
        HEADS = 12
        HEAD_DIM = HIDDEN // HEADS
        NORM = float(np.sqrt(HIDDEN))
        B, S, H = hidden_states.shape

        def heads(x):
            return x.reshape(B, S, HEADS, HEAD_DIM).transpose(0, 2, 1, 3)
        q = heads(hidden_states @ Wq + bq)
        k = heads(hidden_states @ Wk + bk)
        v = heads(hidden_states @ Wv + bv)
        scores = jnp.einsum('bhqd,bhkd->bhqk', q, k) / NORM
        probs = jax.nn.softmax(scores, axis=-1)
        ctx = jnp.einsum('bhqk,bhkd->bhqd', probs, v)
        return ctx.transpose(0, 2, 1, 3).reshape(B, S, H)

    def _L1_ffn_ref(x, W1, b1, W2, b2, Wg, bg):
        import jax, jax.numpy as jnp
        import numpy as np
        E, D, H = (16, 192, 192)
        B, N = (32, 197)
        Bx, Nx, Dx = x.shape
        t = x.reshape(-1, Dx)
        logits = t @ Wg.T + bg
        idx = jnp.argmax(logits, axis=-1)
        out = jnp.zeros_like(t)
        for e in range(W1.shape[0]):
            mask = (idx == e).astype(t.dtype)[:, None]
            h = jax.nn.gelu(t @ W1[e].T + b1[e], approximate=False)
            y = h @ W2[e].T + b2[e]
            out = out + mask * y
        return out.reshape(Bx, Nx, Dx)

    def _gn(v, G=32, eps=1e-05):
        B_, H_, W_, C_ = v.shape
        g = v.reshape(B_, H_, W_, G, C_ // G)
        m = jnp.mean(g, axis=(1, 2, 4), keepdims=True)
        s = jnp.var(g, axis=(1, 2, 4), keepdims=True)
        return ((g - m) / jnp.sqrt(s + eps)).reshape(v.shape)

    def _ln_c(v, eps=1e-06):
        m = jnp.mean(v, axis=-1, keepdims=True)
        s = jnp.var(v, axis=-1, keepdims=True)
        return (v - m) / jnp.sqrt(s + eps)

    def _ln_t(v, eps=1e-05):
        m = jnp.mean(v, axis=-1, keepdims=True)
        s = jnp.var(v, axis=-1, keepdims=True)
        return (v - m) / jnp.sqrt(s + eps)

    def _to_tokens(v):
        B_, H_, W_, C_ = v.shape
        return v.reshape(B_, H_ * W_, C_)

    def _from_tokens(t, like):
        return t.reshape(like.shape)
    x = x + _L0_conv_ref(_gn(x), L0_conv_qkv_w, L0_conv_qkv_b, L0_conv_proj_w, L0_conv_proj_b, L0_conv_rel_pos_h, L0_conv_rel_pos_w)
    t = _to_tokens(x)
    t = t + _L1_attn_ref(_ln_t(t), L1_attn_Wq, L1_attn_bq, L1_attn_Wk, L1_attn_bk, L1_attn_Wv, L1_attn_bv)
    t = t + _L1_ffn_ref(_ln_t(t), L1_ffn_W1, L1_ffn_b1, L1_ffn_W2, L1_ffn_b2, L1_ffn_Wg, L1_ffn_bg)
    x = _from_tokens(t, x)
    return x

_drawn_inputs = setup_inputs


def setup_inputs(seed=0):
    import zlib

    import numpy as np

    out = dict(_drawn_inputs(seed))
    spreads = {'L0_conv_qkv_b': (0.0, 0.1), 'L0_conv_proj_b': (0.0, 0.1), 'L1_ffn_bg': (0.0, 0.1)}
    factors = {'L0_conv_qkv_w': 8.0,
     'L0_conv_rel_pos_h': 8.0,
     'L0_conv_rel_pos_w': 8.0,
     'L1_attn_Wq': 8.0,
     'L1_attn_bq': 64.0,
     'L1_attn_Wk': 8.0,
     'L1_attn_bk': 64.0,
     'L1_ffn_b1': 8.0,
     'L1_ffn_b2': 2.785,
     'L1_attn_bv': 2.683}
    for name, (base, spread) in spreads.items():
        noise = np.random.default_rng([zlib.crc32(name.encode()), seed]).standard_normal(out[name].shape)
        drawn = base * np.exp(spread * noise) if base else spread * noise
        out[name] = jnp.asarray(drawn.astype(out[name].dtype))
    for name, factor in factors.items():
        out[name] = (out[name] * factor).astype(out[name].dtype)
    return out
```

```python
from contextlib import ExitStack

import concourse.bass as bass
import numpy as np
from concourse import mybir

F32 = mybir.dt.float32
F16 = mybir.dt.float16
I32 = mybir.dt.int32
ALU = mybir.AluOpType
ACT = mybir.ActivationFunctionType
AX = mybir.AxisListType

P = 128
B, HI, WI, C = 8, 32, 32, 192
L = HI * WI
T = B * L
NH, HD = 12, 16
GH = 4
NG = NH // GH
STEPS = B * NG
CC = C // 2
KT = L // P
QH = L // 512
VW = 2 * HD
REL = HI + WI
PAIR = 2 * L
ROUNDS = T // PAIR
NCH = 3
GROUPS = 32
MAXSCALE = 64.0
E_N = 16


def spread(n, blocks):
    return [list(range(n * b // blocks, n * (b + 1) // blocks)) for b in range(blocks)]


def make_identity(nc, pool, ident, done):
    nc.gpsimd.memset(ident[:, :], 0.0).then_inc(done, 1)
    pool.wait_ge(done, 1)
    nc.gpsimd.affine_select(out=ident[:, :], in_=ident[:, :], compare_op=ALU.not_equal, fill=1.0,
                            base=0, pattern=[[-1, P]], channel_multiplier=1).then_inc(done, 1)


def attention(nc, name, rel, scale, QK, RL, VN, ON, onehot_dram):
    KQ = (3 if rel else 4) * HD
    R = KQ + (REL if rel else 1)
    NBUF = 3
    BLK = QH * KT
    UNITS = GH * KT
    HALVES = 2 * UNITS
    MAXBLK = BLK - 3
    with ExitStack() as ctx:
        def sb(n, shape, dt):
            return ctx.enter_context(nc.sbuf_tensor(f"{name}_{n}", shape, dt))

        def sem(n):
            return ctx.enter_context(nc.semaphore(f"{name}_{n}"))

        A = [sb(f"qrows{i}", [R + 1, GH, L], F16) for i in range(NBUF)]
        K = [sb(f"krows{i}", [R + 1, GH, L], F16) for i in range(NBUF)]
        V = [sb(f"v{i}", [P, KT, GH, VW], F32) for i in range(NBUF)]
        if rel:
            RLO = [sb(f"rello{i}", [P, GH // 2, L], F16) for i in range(NBUF)]
            E = sb("onehot", [P, L], F16)
        PT = sb("probs", [P, 2, GH, 512], F32)
        MX = [sb(f"halfmax{i}", [P, UNITS, 2], F32) for i in range(NBUF)]
        MC = sb("rowmax", [P, UNITS], F32)
        MT = sb("rowmaxT", [UNITS, P], F16)
        OT = sb("outT", [P, QH, 512], F32)
        RC = sb("recip", [P, 4 * GH, 1], F32)
        OS = sb("out", [P, QH, 4 * GH, HD], F32)
        ident = sb("ident", [P, P], F32)
        psS = ctx.enter_context(nc.psum_tensor(f"{name}_psS", [P, 4, 512], F32))
        psR = ctx.enter_context(nc.psum_tensor(f"{name}_psR", [P, 3, 512], F32))
        psO = ctx.enter_context(nc.psum_tensor(f"{name}_psO", [P, 512], F32))

        const_done = sem("const_done")
        const_dma = sem("const_dma")
        loaded = [sem(f"loaded{i}") for i in range(NBUF)]
        mrow = sem("mrow")
        scores = sem("scores")
        exped = sem("exped")
        pvdone = sem("pvdone")
        ring_full = sem("ring_full")
        ring_free = sem("ring_free")
        maxed = sem("maxed")
        otc = sem("otc")
        recips = sem("recips")
        stored = [sem(f"stored{i}") for i in range(QH)]

        NL = 8 + 1 if not rel else 6 + 1 + 2 + 4
        LB = 16 * NL
        PER_BLK = HALVES // BLK
        EARLY = PER_BLK * (BLK - MAXBLK)

        def jobs_of(g, last):
            after = [[] for _ in range(BLK + 1)]
            for blk in range(BLK):
                offset, u = (1, EARLY + PER_BLK * blk) if blk < MAXBLK else (2, PER_BLK * (blk - MAXBLK))
                if not (last and g + offset >= NG):
                    after[blk] += [("max", u + i, offset) for i in range(PER_BLK)]
            if not (last and g == NG - 1):
                after[MAXBLK].insert(2, ("rows",))
            after[KT + 2].append(("back", 0, 0))
            if g > 0:
                after[2].append(("back", -1, 1))
            if g == NG - 1:
                after[BLK].append(("back", 0, 1))
            return after

        PROLOGUE = HALVES + 1 + EARLY
        FIRST = [("max", u, 0) for u in range(HALVES)] + [("rows",)] + [("max", u, 1) for u in range(EARLY)]

        def number(last):
            at, out = 0, []
            for g in range(NG):
                after = []
                for js in jobs_of(g, last):
                    after.append([(at + n, j) for n, j in enumerate(js)])
                    at += len(js)
                out.append(after)
            return out, at

        JOBS, PER_B = number(False)
        JOBS_LAST, _ = number(True)
        assert PER_B % 3 == 0

        def back_number(jobs, g, qh):
            for gg in range(NG):
                for js in jobs[gg]:
                    for n, j in js:
                        if j[0] == "back" and gg + j[1] == g and j[2] == qh:
                            return n
            raise ValueError

        def rows_number(jobs, g):
            return next(n for n, j in jobs[g][MAXBLK] if j[0] == "rows")

        block = ctx.enter_context(nc.Block())

        @block.gpsimd
        def _(pool):
            make_identity(nc, pool, ident, const_done)

        @block.sync
        def _(sp):
            def load(b, g, buf):
                def rows(c0, part):
                    c = c0 + HD * GH * g
                    return QK[b, part, c:c + HD * GH, :].rearrange("(h d) t -> d h t", h=GH)

                s = b * NG + g
                for n, (pq, pk) in enumerate(((0, 0), (0, 1), (1, 0), (1, 1))[:KQ // HD]):
                    sp.dma_start(A[buf][HD * n:HD * (n + 1), :, :], rows(0, pq)).then_inc(loaded[buf], 16)
                    sp.dma_start(K[buf][HD * n:HD * (n + 1), :, :], rows(C, pk)).then_inc(loaded[buf], 16)
                sp.dma_start(V[buf][:, :, :, :], VN[s]).then_inc(loaded[buf], 16)
                if rel:
                    for hw in range(2):
                        src = RL[s, 0, hw].rearrange("(k h) t -> k h t", h=GH)
                        sp.dma_start(A[buf][KQ + 32 * hw:KQ + 32 * hw + 32, :, :], src).then_inc(loaded[buf], 16)
                        for r in range(2):
                            src = RL[s, 1, hw].rearrange("(k a r) t -> r k a t", r=2, a=2)[r]
                            sp.dma_start(RLO[buf][64 * r + 32 * hw:64 * r + 32 * hw + 32, :, :], src)\
                              .then_inc(loaded[buf], 16)

            def row_of_maxima(buf, free):
                sp.wait_ge(ring_free, free)
                for h in range(GH):
                    sp.dma_start(A[buf][R:R + 1, h, :].rearrange("o (t p) -> o t p", p=P),
                                 MT[KT * h:KT * h + KT, :]).then_inc(mrow, 16)

            def store(b, g, qh, jobs):
                sp.wait_ge(ring_free, PROLOGUE + b * PER_B + back_number(jobs, g, qh) + 4)
                dst = ON[bass.ds(b * L + qh * 512, 512), GH * HD * g:GH * HD * (g + 1)]
                sp.dma_start(dst.rearrange("(t p) c -> p t c", p=P),
                             OS[:, qh, :, :].rearrange("p (t h) d -> p t (h d)", t=4)).then_inc(stored[qh], 16)

            for qh in range(QH):
                nc.sync.sem_inc(stored[qh], 16)
            for i in range(NBUF):
                for h in range(GH):
                    if rel:
                        sp.dma_start(K[i][KQ:R, h, :], onehot_dram[0:REL, :]).then_inc(const_dma, 16)
                    else:
                        sp.dma_start(K[i][KQ:R, h, :], onehot_dram[REL + 1:REL + 2, :]).then_inc(const_dma, 16)
                        sp.dma_start(A[i][KQ:R, h, :], onehot_dram[REL + 1:REL + 2, :]).then_inc(const_dma, 16)
                    sp.dma_start(K[i][R:R + 1, h, :], onehot_dram[REL:REL + 1, :]).then_inc(const_dma, 16)
            if rel:
                for r in range(2):
                    sp.dma_start(E[64 * r:64 * r + 64, :], onehot_dram[0:REL, :]).then_inc(const_dma, 16)
            load(0, 0, 0)
            load(0, 1, 1)
            row_of_maxima(0, HALVES + 4)

            def step(b, g, jobs, last):
                if not (last and g > 0):
                    sp.wait_ge(pvdone, b * (NG * BLK) + g * BLK + 2)
                    load(b if g == 0 else b + 1, 2 if g == 0 else g - 1, (g + 2) % NBUF)
                if g > 0:
                    store(b, g - 1, 1, jobs)
                store(b, g, 0, jobs)
                if not (last and g == NG - 1):
                    row_of_maxima((g + 1) % NBUF, PROLOGUE + b * PER_B + rows_number(jobs, g) + 4)
                if g == NG - 1:
                    store(b, g, 1, jobs)

            with sp.Fori(0, B - 1) as b:
                for g in range(NG):
                    step(b, g, JOBS, False)
            for g in range(NG):
                step(B - 1, g, JOBS_LAST, True)
            for qh in range(QH):
                sp.wait_ge(stored[qh], 16 * STEPS + 16)

        @block.tensor
        def _(pe):
            def job(jn, j, base, slot, g, halves, rows):
                pe.wait_ge(ring_free, base + jn + 1)
                if j[0] == "max":
                    u, half = j[1] // 2, j[1] % 2
                    h, qt, buf = u // KT, u % KT, (g + j[2]) % NBUF
                    mm = nc.tensor.matmul(psR[:, slot, :], A[buf][0:R, h, P * qt:P * qt + P],
                                          K[buf][0:R, h, 512 * half:512 * half + 512], start=True, stop=True)
                elif j[0] == "rows":
                    pe.wait_ge(maxed, rows + 1)
                    mm = nc.tensor.transpose(psR[0:UNITS, slot, 0:P], MC[:, :], ident[:, :])
                else:
                    pe.wait_ge(otc, halves + QH * j[1] + j[2] + 2)
                    for qt in range(4):
                        mm = nc.tensor.transpose(psR[:, slot, P * qt:P * qt + P],
                                                 OT[:, j[2], P * qt:P * qt + P], ident[:, :])
                mm.then_inc(ring_full, 1)

            def scores_pair(buf, kt, qh, pair, n, pairs):
                pe.wait_ge(exped, pairs + n + 1)
                for j in range(2):
                    h = 2 * pair + j
                    mm = nc.tensor.matmul(psS[:, (2 * n + j) % 4, :], K[buf][0:R + 1, h, P * kt:P * kt + P],
                                          A[buf][0:R + 1, h, 512 * qh:512 * qh + 512], start=True, stop=not rel)
                if rel:
                    for j in range(2):
                        mm = nc.tensor.matmul(psS[:, (2 * n + j) % 4, :],
                                              E[64 * j:64 * j + 64, P * kt:P * kt + P],
                                              RLO[buf][64 * j:64 * j + 64, pair, 512 * qh:512 * qh + 512],
                                              start=False, stop=True)
                mm.then_inc(scores, 1)

            def pv(buf, blk, blks, halves):
                kt, qh = blk % KT, blk // KT
                pe.wait_ge(exped, 2 * (blks + blk + 1) + 2)
                if kt == 0:
                    pe.wait_ge(otc, halves + qh + 1)
                for h in range(GH):
                    mm = nc.tensor.matmul(psO[32 * h:32 * h + 32, :], V[buf][:, kt, h, :], PT[:, blk % 2, h, :],
                                          start=(kt == 0), stop=(kt == KT - 1))
                mm.then_inc(pvdone, 1)

            def step(b, g, jobs, last):
                s = b * NG + g
                blks, halves, base = s * BLK, s * QH, PROLOGUE + b * PER_B
                pe.wait_ge(mrow, s * (16 * GH) + 16 * GH)
                for blk in range(BLK):
                    if blk == MAXBLK and not (last and g + 2 >= NG):
                        pe.wait_ge(loaded[(g + 2) % NBUF], b * LB + ((g + 2) // NG + 1) * LB)
                    js = jobs[g][blk]
                    for pair in range(2):
                        scores_pair(g, blk % KT, blk // KT, pair, 2 * blk + pair, 2 * blks)
                        for jn, j in js[:len(js) // 2] if pair == 0 else js[len(js) // 2:]:
                            job(jn, j, base, (PROLOGUE + jn) % 3, g, halves, s + 1)
                    if blk >= 1:
                        pv(g, blk - 1, blks, halves)
                    elif g > 0:
                        pv(g - 1, BLK - 1, blks - BLK, halves - QH)
                if g == NG - 1:
                    pv(g, BLK - 1, blks, halves)
                    for jn, j in jobs[g][BLK]:
                        job(jn, j, base, (PROLOGUE + jn) % 3, g, halves, s + 1)

            pe.wait_ge(const_done, 2)
            pe.wait_ge(const_dma, 16 * (NBUF * GH * (2 if rel else 3) + (2 if rel else 0)))
            pe.wait_ge(loaded[0], LB)
            for n, j in enumerate(FIRST):
                if n == HALVES + 1:
                    pe.wait_ge(loaded[1], LB)
                job(n, j, 0, n % 3, 0, 0, 0)
            with pe.Fori(0, B - 1) as b:
                for g in range(NG):
                    step(b, g, JOBS, False)
            for g in range(NG):
                step(B - 1, g, JOBS_LAST, True)

        @block.scalar
        def _(act):
            nc.scalar.sem_inc(exped, 2)
            nc.scalar.sem_inc(otc, 1)

            def copy_out(b, g, qh, jobs):
                act.wait_ge(pvdone, b * (NG * BLK) + g * BLK + KT * (qh + 1) + 2)
                before = back_number(JOBS, NG - 1, qh) - PER_B if g == 0 else back_number(jobs, g - 1, qh)
                act.wait_ge(ring_free, b * PER_B + (PROLOGUE + before + 4))
                nc.scalar.copy(OT[:, qh, :], psO[:, :]).then_inc(otc, 1)

            def step(b, g, jobs):
                s = b * NG + g
                for n in range(2 * BLK):
                    blk, pair = n // 2, n % 2
                    act.wait_ge(scores, s * (2 * BLK) + n + 1)
                    act.wait_ge(pvdone, s * BLK + blk + 1)
                    b0 = 2 * n % 4
                    nc.scalar.activation(PT[:, blk % 2, 2 * pair:2 * pair + 2, :], psS[:, b0:b0 + 2, :], ACT.Exp,
                                         scale=scale).then_inc(exped, 1)
                    if n == 1 and g > 0:
                        copy_out(b, g - 1, 1, jobs)
                    if n == 2 * KT + 1:
                        copy_out(b, g, 0, jobs)
                if g == NG - 1:
                    copy_out(b, g, 1, jobs)

            with act.Fori(0, B - 1) as b:
                for g in range(NG):
                    step(b, g, JOBS)
            for g in range(NG):
                step(B - 1, g, JOBS_LAST)

        @block.vector
        def _(dve):
            nc.vector.sem_inc(pvdone, 2)
            nc.vector.sem_inc(ring_free, 3)

            def job(jn, j, base, slot, g, steps):
                dve.wait_ge(ring_full, base + jn + 1)
                if j[0] == "max":
                    mx = MX[(g + j[2]) % NBUF]
                    nc.vector.tensor_reduce(mx[:, j[1] // 2, j[1] % 2:j[1] % 2 + 1], psR[:, slot, :], AX.X, ALU.max)\
                        .then_inc(ring_free, 1)
                    if j[1] == HALVES - 1:
                        dve.wait_ge(ring_free, base + jn + 4)
                        nc.vector.tensor_tensor(MC[:, :], mx[:, :, 0], mx[:, :, 1], ALU.max).then_inc(maxed, 1)
                elif j[0] == "rows":
                    if steps is not None:
                        dve.wait_ge(mrow, steps * (16 * GH) + 16 * GH)
                    nc.vector.tensor_scalar(MT[:, :], psR[0:UNITS, slot, 0:P], -1.0 / MAXSCALE, None, ALU.mult)\
                        .then_inc(ring_free, 1)
                else:
                    qh, half = j[2], steps * QH + j[1] * QH + j[2]
                    o = psR[:, slot, :].rearrange("p (x v) -> p x v", v=VW)
                    dve.wait_ge(ring_free, base + jn + 3)
                    nc.vector.reciprocal(RC[:, :, :], o[:, :, HD:HD + 1]).then_inc(recips, 1)
                    dve.wait_ge(recips, half + 1)
                    dve.wait_ge(stored[qh], steps * 16 + (16 * j[1] + 16))
                    nc.vector.tensor_tensor(OS[:, qh, :, :], o[:, :, 0:HD], RC[:, :, :].to_broadcast([P, 4 * GH, HD]),
                                            ALU.mult).then_inc(ring_free, 1)

            for n, j in enumerate(FIRST):
                job(n, j, 0, n % 3, 0, None)

            def step(b, g, jobs):
                for js in jobs[g]:
                    for jn, j in js:
                        job(jn, j, PROLOGUE + b * PER_B, (PROLOGUE + jn) % 3, g, b * NG + g)

            with dve.Fori(0, B - 1) as b:
                for g in range(NG):
                    step(b, g, JOBS)
            for g in range(NG):
                step(B - 1, g, JOBS_LAST)


def project(nc, name, first, IN, W, CONST, QK, VN, RL=None, ON=None, X2=None):
    NT = PAIR // P
    RX = 8
    EPS = 1e-5
    with ExitStack() as ctx:
        def sb(n, shape, dt=F32):
            return ctx.enter_context(nc.sbuf_tensor(f"{name}_{n}", shape, dt))

        def ps(n, shape):
            return ctx.enter_context(nc.psum_tensor(f"{name}_{n}", shape, F32))

        def sem(n):
            return ctx.enter_context(nc.semaphore(f"{name}_{n}"))

        XN = sb("xnT", [CC, 2, PAIR])
        QF = sb("qk", [P, NCH, PAIR])
        HL = [sb(f"half{i}", [P, NCH, PAIR], F16) for i in range(2)]
        VT = sb("v", [P, NT, NH, VW])
        WQK = sb("wqk", [CC, 2, 2 * C])
        WV = sb("wv", [CC, 2, C])
        BQK = sb("bqk", [P, NCH])
        BV2 = sb("bv", [P, 2 * C])
        SC = sb("sc", [P, NCH])
        psQ = ps("psQ", [P, 2, 512])
        psV = ps("psV", [P, 2, 512])
        psR = ps("psR", [P, 4, 512])

        wload = sem("wload")
        preset = sem("preset")
        xload = sem("xload")
        xnorm = sem("xnorm")
        qps = sem("qps")
        qf = sem("qf")
        vps = sem("vps")
        vt = sem("vt")
        hi = sem("hi")
        lo = sem("lo")
        qkst = sem("qkst")
        vst = sem("vst")
        rsq = sem("rsq")
        gate = sem("gate")
        if first:
            X = sb("xT", [CC, 2, PAIR])
            G = sb("groupmean", [CC, CC])
            ST = sb("stats", [CC, 4, 2, 6])
            MV = sb("meanvar", [CC, 4, 2])
            D = sb("between", [CC, 4])
            D2 = sb("spread", [CC, 4])
            GM = sb("gmean", [CC, 4])
            VE = sb("variance", [CC, 4])
            HALF = sb("half", [CC, 4])
            RS = sb("rstd", [CC, 4])
            RT = sb("relT", [P, 2, 2 * HI - 1, GH])
            RH = [[sb(f"rel{g}_{i}", [P, 2, PAIR], F16) for i in range(2)] for g in range(NG)]
            dchain = sem("dchain")
            DC = 7
            gps = sem("gps")
            rps = sem("rps")
            rhi = sem("rhi")
            rlo = sem("rlo")
            rst = sem("rst")
            NR = NG * 2 * (HI // RX)
        else:
            O = sb("attn", [P, NT, C])
            X = sb("x", [P, NT, C])
            OTs = sb("attnT", [CC, 2, 2, P])
            XM = sb("xm", [P, NT, C])
            WP = sb("wproj", [CC, 2, C])
            BP = sb("bproj", [P, C])
            ST = sb("stats", [P, NT, 6])
            MV = sb("meanvar", [P, NT, 2])
            VE = sb("variance", [P, NT])
            HALF = sb("half", [P, NT])
            RS = sb("rstd", [P, NT])
            ident = sb("ident", [P, P])
            made = sem("made")
            oload = sem("oload")
            xb = sem("xb")
            otp = sem("otp")
            ots = sem("ots")
            pps = sem("pps")
            x2 = sem("x2")
            st = sem("st")
            xm = sem("xm")
            xtp = sem("xtp")
            x2st = sem("x2st")
        LAG = 8
        PIECES = 4 if first else NT
        NW = 16 * (6 + (1 + 2 * GH * 2 if first else 2))

        def rel_views(g, half, hw, x0, bank):
            src = psR[:, bank, :].rearrange("p (b x y) -> p b x y", b=2, x=RX)
            dst = RH[g][half][:, hw, :].rearrange("p (b h w) -> p b h w", b=2, h=HI)
            if hw == 0:
                return [dst[:, b, x0:x0 + RX, :] for b in range(2)], [src[:, b] for b in range(2)]
            return ([dst[:, b, :, x0:x0 + RX] for b in range(2)],
                    [src[:, b].rearrange("p x y -> p y x") for b in range(2)])

        block = ctx.enter_context(nc.Block())

        @block.sync
        def _(sp):
            for dst, src in ((WQK, W["wqk"].rearrange("(c p) n -> p c n", p=CC)),
                             (WV, W["wv"].rearrange("(c p) n -> p c n", p=CC)),
                             (SC, CONST["sc"])):
                sp.dma_start(dst[:], src).then_inc(wload, 16)
            with nc.allow_non_contiguous_dma(reason="biases, once"):
                sp.dma_start(BQK[:, :], W["bqk"].rearrange("(m p) -> p m", p=P)).then_inc(wload, 16)
            for t in range(2):
                sp.dma_start(BV2[:, C * t:C * t + C], W["bv"].rearrange("(o n) -> o n", o=1).to_broadcast([P, C]))\
                  .then_inc(wload, 16)
            if first:
                sp.dma_start(G[:, :], CONST["group"]).then_inc(wload, 16)
                sp.wait_ge(preset, 3)
                for r in range(2):
                    for h in range(GH):
                        for hw in range(2):
                            row = 64 * r + HD * h
                            with nc.allow_non_contiguous_dma(reason="a small table, once"):
                                sp.dma_start(RT[row:row + HD, hw, :, h], W["relT"][hw]).then_inc(wload, 16)
            else:
                sp.dma_start(WP[:], W["proj_w"].rearrange("(c p) n -> p c n", p=CC)).then_inc(wload, 16)
                sp.dma_start(BP[:, :], W["proj_b"].rearrange("(o n) -> o n", o=1).to_broadcast([P, C]))\
                  .then_inc(wload, 16)

            nc.sync.sem_inc(qkst, 16)
            nc.sync.sem_inc(vst, 16)
            nc.sync.sem_inc(rst if first else x2st, 16)
            with sp.Fori(0, ROUNDS) as j:
                if not first:
                    for q in range(4):
                        sp.wait_ge(x2, j * NT + 4 * (q + 1) + 2)
                        nc.sync.sem_inc(gate, 1)
                        dst = X2[bass.ds(j * PAIR + q * 512, 512), :].rearrange("(t p) c -> p t c", p=P)
                        sp.dma_start(dst, X[:, 4 * q:4 * q + 4, :]).then_inc(x2st, 16)
                for m in range(NCH):
                    for half, s in ((0, hi), (1, lo)):
                        sp.wait_ge(s, j * NCH + m + 1 + half)
                        nc.sync.sem_inc(gate, 1)
                        dst = QK[bass.ds(2 * j, 2), half, P * m:P * m + P, :].rearrange("b c t -> c b t")
                        sp.dma_start(dst, HL[half][:, m, :].rearrange("p (b t) -> p b t", b=2)).then_inc(qkst, 16)
                sp.wait_ge(vt, j * (NT // 2) + NT // 2 + 2)
                nc.sync.sem_inc(gate, 1)
                for b in range(2):
                    for g in range(NG):
                        sp.dma_start(VN[j * (2 * NG) + (b * NG + g)],
                                     VT[:, b * KT:b * KT + KT, GH * g:GH * g + GH, :]).then_inc(vst, 16)
                if first:
                    for g in range(NG):
                        sp.wait_ge(rlo, j * NR + (NR // NG) * (g + 1) + 4)
                        nc.sync.sem_inc(gate, 1)
                        for half in range(2):
                            for b in range(2):
                                dst = RL[j * (2 * NG) + (b * NG + g), half].rearrange("w c t -> c w t")
                                sp.dma_start(dst, RH[g][half][:, :, b * L:b * L + L]).then_inc(rst, 16)
            sp.wait_ge(qkst, ROUNDS * 96 + 16)
            sp.wait_ge(vst, ROUNDS * 96 + 16)
            if first:
                sp.wait_ge(rst, ROUNDS * 192 + 16)
            else:
                sp.wait_ge(x2st, ROUNDS * 64 + 16)

        @block.gpsimd
        def _(pool):
            nc.gpsimd.memset(VT[:, :, :, :], 1.0).then_inc(preset, 1)
            nc.gpsimd.memset(HALF[:, :], -0.5).then_inc(preset, 1)
            if first:
                nc.gpsimd.memset(RT[:, :, :, :], 0.0).then_inc(preset, 1)
            else:
                make_identity(nc, pool, ident, made)
            pool.wait_ge(wload, NW)
            pool.wait_ge(preset, 3 if first else 2)
            with pool.Fori(0, ROUNDS) as j:
                if first:
                    pool.wait_ge(xnorm, j * PIECES + 1)
                    nc.gpsimd.sem_inc(gate, 1)
                    src = IN[:, bass.ds(j * PAIR, PAIR)].rearrange("(c p) t -> p c t", p=CC)
                    pool.dma_start(X[:, :, :], src).then_inc(xload, 16)
                    pool.wait_ge(dchain, j * DC + DC)
                    nc.gpsimd.tensor_tensor(RS[:, :], VE[:, :], HALF[:, :], ALU.pow).then_inc(rsq, 1)
                else:
                    pool.wait_ge(x2st, j * 64 + 16)
                    pool.wait_ge(xnorm, j * PIECES + 1)
                    nc.gpsimd.sem_inc(gate, 1)
                    for dst, src, s in ((O, ON, oload), (X, IN, xload)):
                        pool.dma_start(dst[:, :, :], src[bass.ds(j * PAIR, PAIR), :]
                                       .rearrange("(t p) c -> p t c", p=P)).then_inc(s, 16)
                    pool.wait_ge(xload, j * 16 + 16)
                    nc.gpsimd.tensor_tensor(X[:, :, :], X[:, :, :], BP[:, :].rearrange("p (o c) -> p o c", o=1)
                                            .to_broadcast([P, NT, C]), ALU.add).then_inc(xb, 1)
                    for q in range(NT // 4):
                        pool.wait_ge(st, j * (3 * NT // 4) + (3 * q + 3))
                        nc.gpsimd.tensor_tensor(RS[:, 4 * q:4 * q + 4], VE[:, 4 * q:4 * q + 4],
                                                HALF[:, 4 * q:4 * q + 4], ALU.pow).then_inc(rsq, 1)

        @block.tensor
        def _(pe):
            pe.wait_ge(wload, NW)
            if not first:
                pe.wait_ge(made, 2)

            def group_mean(n, j, dst, src):
                pe.wait_ge(dchain, j * DC + n)
                nc.tensor.matmul(dst[0:CC, 0:4], G[:, :], src, start=True, stop=True).then_inc(gps, 1)

            def turn_attn(i, j):
                if i == 0:
                    pe.wait_ge(oload, j * 16 + 16)
                    pe.wait_ge(qf, j * (4 * NCH) + 2)
                    pe.wait_ge(vt, j * (NT // 2) + 2)
                pe.wait_ge(ots, j * NT + i + 1)
                for c in range(2):
                    mm = nc.tensor.transpose(psQ[0:CC, i % 2, P * c:P * c + P], O[:, i, CC * c:CC * c + CC], ident[:, :])
                mm.then_inc(otp, 1)

            def proj(i, j):
                pe.wait_ge(ots, j * NT + i + 3)
                pe.wait_ge(x2, j * NT + i + 1)
                for c in range(2):
                    mm = nc.tensor.matmul(psV[:, i % 2, 0:C], OTs[:, i % 2, c, :], WP[:, c, :], start=(c == 0), stop=(c == 1))
                mm.then_inc(pps, 1)

            def turn_x(i, j):
                pe.wait_ge(xm, j * NT + i + 1)
                if i >= 4:
                    pe.wait_ge(xnorm, j * NT + i - 2)
                for c in range(2):
                    mm = nc.tensor.transpose(psR[0:CC, i % 4, P * c:P * c + P], XM[:, i, CC * c:CC * c + CC],
                                             ident[:, :])
                mm.then_inc(xtp, 1)

            with pe.Fori(0, ROUNDS) as j:
                if first:
                    group_mean(2, j, psV[:, 0, :], MV[:, :, 0])
                    group_mean(6, j, psV[:, 1, :], D2[:, :])
                else:
                    for i in range(NT + LAG):
                        if i < NT:
                            turn_attn(i, j)
                        if 1 <= i <= NT:
                            proj(i - 1, j)
                        if i >= LAG:
                            turn_x(i - LAG, j)
                pe.wait_ge(xnorm, j * PIECES + PIECES + 1)
                n = 0
                for m in range(NCH):
                    for q in range(PAIR // 512):
                        pe.wait_ge(qf, j * (4 * NCH) + (n + 1))
                        for c in range(2):
                            mm = nc.tensor.matmul(psQ[:, n % 2, :], WQK[:, c, P * m:P * m + P],
                                                  XN[:, c, 512 * q:512 * q + 512], start=(c == 0), stop=(c == 1))
                        mm.then_inc(qps, 1)
                        n += 1
                for t in range(NT):
                    if t % 2 == 0:
                        pe.wait_ge(vt, j * (NT // 2) + (t // 2 + 1))
                    for c in range(2):
                        mm = nc.tensor.matmul(psV[:, t // 2 % 2, C * (t % 2):C * (t % 2) + C],
                                              XN[:, c, P * t:P * t + P], WV[:, c, :], start=(c == 0), stop=(c == 1))
                    if t % 2 == 1:
                        mm.then_inc(vps, 1)
                if first:
                    n = 0
                    for g in range(NG):
                        r, m = 64 * (g % 2), g // 2
                        for hw in range(2):
                            q = QF[r:r + 64, m, :].rearrange("p (b h w) -> p b h w", b=2, h=HI)
                            for x0 in range(0, HI, RX):
                                pe.wait_ge(rlo, j * NR + (n + 1))
                                o = psR[:, n % 4, :].rearrange("p (b x y) -> p b x y", b=2, x=RX)
                                for x in range(RX):
                                    xx = x0 + x
                                    mm = nc.tensor.matmul(o[:, :, x, :], RT[r:r + 64, hw, HI - 1 - xx:2 * HI - 1 - xx, :]
                                                          .rearrange("p k h -> p (k h)"),
                                                          q[:, :, xx, :] if hw == 0 else q[:, :, :, xx],
                                                          start=True, stop=True)
                                mm.then_inc(rps, 1)
                                n += 1

        @block.scalar
        def _(act):
            nc.scalar.sem_inc(qf, 2)
            act.wait_ge(wload, NW)
            if not first:
                nc.scalar.sem_inc(ots, 2)
                nc.scalar.sem_inc(xnorm, 1)
            with act.Fori(0, ROUNDS) as j:
                if not first:
                    act.wait_ge(vt, j * (NT // 2) + 2)
                    for i in range(NT + LAG):
                        if i < NT:
                            act.wait_ge(otp, j * NT + i + 1)
                            if i >= 2:
                                act.wait_ge(pps, j * NT + i - 1)
                            nc.scalar.copy(OTs[:, i % 2, :, :], psQ[0:CC, i % 2, 0:2 * P].rearrange("p (c t) -> p c t", c=2))\
                                .then_inc(ots, 1)
                        if i >= LAG:
                            t = i - LAG
                            act.wait_ge(xtp, j * NT + t + 1)
                            nc.scalar.copy(XN[:, :, P * t:P * t + P],
                                           psR[0:CC, t % 4, 0:2 * P].rearrange("p (c t) -> p c t", c=2))\
                                .then_inc(xnorm, 1)
                n = 0
                act.wait_ge(lo, j * NCH + 1)
                if first:
                    act.wait_ge(rlo, j * NR + 4)
                act.wait_ge(qkst, j * 96 + 16)
                for m in range(NCH + 1):
                    for q in range(PAIR // 512 if m < NCH else 0):
                        act.wait_ge(qps, j * (4 * NCH) + (n + 1))
                        nc.scalar.activation(QF[:, m, 512 * q:512 * q + 512], psQ[:, n % 2, :], ACT.Identity,
                                             bias=BQK[:, m:m + 1], scale=1.0).then_inc(qf, 1)
                        n += 1
                    if m > 0:
                        act.wait_ge(qf, j * (4 * NCH) + (4 * m + 2))
                        nc.scalar.activation(HL[0][:, m - 1, :], QF[:, m - 1, :], ACT.Identity,
                                             scale=SC[:, m - 1:m]).then_inc(hi, 1)
                if first:
                    act.wait_ge(rst, j * 192 + 16)
                    n = 0
                    for g in range(NG):
                        for hw in range(2):
                            for x0 in range(0, HI, RX):
                                act.wait_ge(rps, j * NR + (n + 1))
                                dst, src = rel_views(g, 0, hw, x0, n % 4)
                                for b in range(2):
                                    a = nc.scalar.copy(dst[b], src[b])
                                a.then_inc(rhi, 1)
                                n += 1

        @block.vector
        def _(dve):
            nc.vector.sem_inc(vt, 2)
            nc.vector.sem_inc(lo, 1)
            if first:
                nc.vector.sem_inc(xnorm, 1)
                nc.vector.sem_inc(rlo, 4)
            else:
                nc.vector.sem_inc(x2, 2)
            dve.wait_ge(wload, NW)
            dve.wait_ge(preset, 3 if first else 2)

            def group_norm(j):
                n = [0]

                def link(ins):
                    n[0] += 1
                    ins.then_inc(dchain, 1)
                    dve.wait_ge(dchain, j * DC + n[0])

                dve.wait_ge(xload, j * 16 + 16)
                for k in range(4):
                    c, b = k % 2, k // 2
                    for h in range(2):
                        t = b * L + 512 * h
                        ins = nc.vector.bn_stats(ST[:, k, h, :], X[:, c, t:t + 512])
                link(ins)
                nc.vector.sem_inc(gate, 1)
                for k in range(4):
                    ins = nc.vector.bn_aggr(MV[:, k, :], ST[:, k, :, :].rearrange("p h s -> p (h s)"))
                link(ins)
                dve.wait_ge(gps, j * 2 + 1)
                link(nc.vector.tensor_copy(GM[:, :], psV[0:CC, 0, 0:4]))
                link(nc.vector.tensor_tensor(D[:, :], MV[:, :, 0], GM[:, :], ALU.subtract))
                link(nc.vector.tensor_tensor(D2[:, :], D[:, :], D[:, :], ALU.mult))
                link(nc.vector.tensor_tensor(D2[:, :], D2[:, :], MV[:, :, 1], ALU.add))
                dve.wait_ge(gps, j * 2 + 2)
                link(nc.vector.tensor_scalar(VE[:, :], psV[0:CC, 1, 0:4], EPS, None, ALU.add))
                assert n[0] == DC
                dve.wait_ge(rsq, j + 1)
                dve.wait_ge(vt, j * (NT // 2) + 2)
                for k in range(4):
                    c, b = k % 2, k // 2
                    nc.vector.tensor_scalar(XN[:, c, b * L:b * L + L], X[:, c, b * L:b * L + L], GM[:, k:k + 1],
                                            RS[:, k:k + 1], ALU.subtract, ALU.mult).then_inc(xnorm, 1)

            def residual_and_norm(j):
                dve.wait_ge(xb, j + 1)
                for q in range(NT // 4 + 1):
                    tiles = range(4 * q, 4 * q + 4)
                    at = j * (3 * NT // 4) + 3 * q
                    if q < NT // 4:
                        for t in tiles:
                            dve.wait_ge(pps, j * NT + (t + 1))
                            nc.vector.tensor_tensor(X[:, t, :], psV[:, t % 2, 0:C], X[:, t, :], ALU.add).then_inc(x2, 1)
                        dve.wait_ge(x2, j * NT + (4 * q + 4 + 2))
                        for t in tiles:
                            ins = nc.vector.bn_stats(ST[:, t, :], X[:, t, :])
                        ins.then_inc(st, 1)
                        dve.wait_ge(st, at + 1)
                        nc.vector.sem_inc(gate, 1)
                        for t in tiles:
                            ins = nc.vector.bn_aggr(MV[:, t, :], ST[:, t, :])
                        ins.then_inc(st, 1)
                        dve.wait_ge(st, at + 2)
                        nc.vector.tensor_scalar(VE[:, 4 * q:4 * q + 4], MV[:, 4 * q:4 * q + 4, 1], EPS, None, ALU.add)\
                            .then_inc(st, 1)
                    if q > 0:
                        dve.wait_ge(rsq, j * (NT // 4) + q)
                        for t in range(4 * q - 4, 4 * q):
                            nc.vector.tensor_scalar(XM[:, t, :], X[:, t, :], MV[:, t, 0:1], RS[:, t:t + 1],
                                                    ALU.subtract, ALU.mult).then_inc(xm, 1)

            with dve.Fori(0, ROUNDS) as j:
                if first:
                    group_norm(j)
                else:
                    residual_and_norm(j)
                for m in range(NCH):
                    dve.wait_ge(hi, j * NCH + m + 1)
                    if m == 0:
                        dve.wait_ge(qkst, j * 96 + 16)
                    nc.vector.scalar_tensor_tensor(HL[1][:, m, :], QF[:, m, :], SC[:, m:m + 1], HL[0][:, m, :],
                                                   ALU.mult, ALU.subtract).then_inc(lo, 1)
                dve.wait_ge(vst, j * 96 + 16)
                for n in range(NT // 2):
                    dve.wait_ge(vps, j * (NT // 2) + n + 1)
                    nc.vector.tensor_tensor(
                        VT[:, 2 * n:2 * n + 2, :, 0:HD].rearrange("p t h d -> p (t h) d"),
                        psV[:, n % 2, 0:2 * C].rearrange("p (x d) -> p x d", d=HD),
                        BV2[:, :].rearrange("p (x d) -> p x d", d=HD), ALU.add).then_inc(vt, 1)
                if first:
                    n = 0
                    for g in range(NG):
                        for hw in range(2):
                            for x0 in range(0, HI, RX):
                                dve.wait_ge(rhi, j * NR + (n + 1))
                                dst, src = rel_views(g, 1, hw, x0, n % 4)
                                high, _ = rel_views(g, 0, hw, x0, n % 4)
                                for b in range(2):
                                    a = nc.vector.tensor_tensor(dst[b], src[b], high[b], ALU.subtract)
                                a.then_inc(rlo, 1)
                                n += 1


CAP = T
NTILE = T // P + E_N
LIST = E_N * CAP + NTILE * P
CM = C + 2
EMPTY = 1 << 20


def route(nc, name, X2, ON, WG, BG, X3, SLOTS, TILES):
    NT = L // P
    EPS = 1e-5
    with ExitStack() as ctx:
        def sb(n, shape, dt=F32):
            return ctx.enter_context(nc.sbuf_tensor(f"{name}_{n}", shape, dt))

        def ps(n, shape):
            return ctx.enter_context(nc.psum_tensor(f"{name}_{n}", shape, F32))

        def sem(n):
            return ctx.enter_context(nc.semaphore(f"{name}_{n}"))

        O = sb("attn", [P, NT, C])
        X = sb("x", [P, NT, CM])
        XM = sb("xm", [P, NT, C])
        XT = sb("xmT", [CC, 2, L])
        ST = sb("stats", [P, NT, 6])
        MV = sb("meanvar", [P, NT, 2])
        VE = sb("variance", [P, NT, 1])
        HALF = sb("half", [P, NT, 1])
        WGs = sb("wg", [CC, 2, E_N])
        BGs = sb("bg", [P, NT, E_N])
        LG = sb("logits", [P, NT, E_N])
        LM = sb("top", [P, NT, 1])
        EQ = sb("isTop", [P, NT, E_N])
        OH = sb("chosen", [P, NT, E_N])
        OS = sb("chosenSum", [P, E_N])
        RUN = sb("chosenBefore", [P, E_N])
        DESC = sb("descending", [P, NT, E_N])
        EB = sb("expertBase", [P, NT, E_N])
        PW = sb("place", [P, NT, E_N])
        PO = sb("placeOf", [P, NT, 1])
        POI = sb("placeOfInt", [P, NT], I32)
        IDF = sb("tokenIds", [P, NT])
        IDI = sb("tokenIdsInt", [P, NT], I32)
        TRI = sb("before", [P, P])
        ONE = sb("ones", [P, P])
        ident = sb("ident", [P, P])
        FILL = sb("empty", [P, LIST // P], I32)
        NTe = sb("tilesOf", [E_N, 1])
        NTi = sb("tilesOfInt", [E_N, 1], I32)
        NTB = sb("tilesOfWide", [E_N, P])
        UPTO = sb("upto", [E_N, E_N])
        END = sb("tileEnds", [P, E_N])
        GE = sb("past", [P, E_N])
        GEE = sb("pastEnds", [P, E_N])
        JP = sb("tileNumber", [P, 1])
        TL = sb("tileList", [P, 2])
        START = sb("tileStart", [P, 1])
        BASE = sb("tileBase", [P, 1])
        TR = sb("tileRows", [2, P], I32)
        psT = ps("psT", [P, 2, 512])
        psL = ps("psL", [P, 512])
        psK = ps("psK", [P, 512])
        psC = ps("psC", [P, 512])

        made = sem("made")
        wload = sem("wload")
        filled = sem("filled")
        load = sem("load")
        x3 = sem("x3")
        x3st = sem("x3st")
        ch = sem("ch")
        xtp = sem("xtp")
        xts = sem("xts")
        lg = sem("lg")
        rk = sem("rk")
        scat = sem("scat")
        idn = sem("idn")
        fin = sem("fin")
        out = sem("out")
        rsq = sem("rsq")
        gate = sem("gate")
        CH, CH0 = 19, 15
        NMADE = 12

        block = ctx.enter_context(nc.Block())

        @block.sync
        def _(sp):
            nc.sync.sem_inc(x3st, 16)
            sp.dma_start(WGs[:], WG.rearrange("(c p) n -> p c n", p=CC)).then_inc(wload, 16)
            for t in range(NT):
                sp.dma_start(BGs[:, t, :], BG.rearrange("(o n) -> o n", o=1).to_broadcast([P, E_N])).then_inc(wload, 16)
            sp.wait_ge(made, NMADE)
            sp.dma_start(SLOTS.rearrange("(p n) o -> p (n o)", p=P), FILL[:, :]).then_inc(filled, 16)
            with sp.Fori(0, B) as b:
                sp.wait_ge(x3, b + 1)
                sp.wait_ge(x3st, b * 16 + 16)
                sp.wait_ge(ch, b * CH + (5 - CH + CH0))
                nc.sync.sem_inc(gate, 1)
                for dst, src in ((O, ON), (X, X2)):
                    sp.dma_start(dst[:, :, 0:C], src[bass.ds(b * L, L), :].rearrange("(t p) c -> p t c", p=P))\
                      .then_inc(load, 16)
                sp.wait_ge(rsq, b + 1)
                nc.sync.sem_inc(gate, 1)
                sp.wait_ge(ch, b * CH + 3 + CH0)
                nc.sync.sem_inc(gate, 1)
                sp.dma_start(X3[bass.ds(b * L, L), :].rearrange("(t p) c -> p t c", p=P), X[:, :, :])\
                  .then_inc(x3st, 16)
            sp.wait_ge(x3st, B * 16 + 16)
            sp.wait_ge(fin, 18)
            sp.dma_start(TILES, TR[:, :]).then_inc(out, 16)
            sp.wait_ge(out, 16)

        @block.gpsimd
        def _(pool):
            nc.gpsimd.sem_inc(idn, 1)
            make_identity(nc, pool, ident, made)
            nc.gpsimd.memset(ONE[:, :], 1.0).then_inc(made, 1)
            pool.wait_ge(made, 3)
            nc.gpsimd.affine_select(out=TRI[:, :], in_=ONE[:, :], compare_op=ALU.is_gt, fill=0.0, base=0,
                                    pattern=[[1, P]], channel_multiplier=-1).then_inc(made, 1)
            nc.gpsimd.affine_select(out=UPTO[:, :], in_=ONE[0:E_N, 0:E_N], compare_op=ALU.is_ge, fill=0.0, base=0,
                                    pattern=[[1, E_N]], channel_multiplier=-1).then_inc(made, 1)
            exact = dict(allow_small_or_imprecise_dtypes=True)
            nc.gpsimd.iota(DESC[:, :, :], [[0, NT], [-1, E_N]], base=E_N, channel_multiplier=0, **exact)\
                .then_inc(made, 1)
            nc.gpsimd.iota(EB[:, :, :], [[0, NT], [CAP, E_N]], base=0, channel_multiplier=0, **exact).then_inc(made, 1)
            nc.gpsimd.iota(IDF[:, :], [[P, NT]], base=0, channel_multiplier=1, **exact).then_inc(made, 1)
            nc.gpsimd.iota(JP[:, :], [[0, 1]], base=0, channel_multiplier=1, **exact).then_inc(made, 1)
            nc.gpsimd.memset(RUN[:, :], 0.0).then_inc(made, 1)
            nc.gpsimd.memset(HALF[:, :, :], -0.5).then_inc(made, 1)
            nc.gpsimd.memset(FILL[:, :], EMPTY).then_inc(made, 1)
            pool.wait_ge(filled, 16)
            pool.wait_ge(made, NMADE)
            with pool.Fori(0, B) as b:
                pool.wait_ge(ch, b * CH + 4 + CH0)
                nc.gpsimd.tensor_tensor(X[:, :, C + 1:C + 2], VE[:, :, :], HALF[:, :, :], ALU.pow).then_inc(rsq, 1)
                pool.wait_ge(ch, b * CH + 16 + CH0)
                nc.gpsimd.sem_inc(gate, 1)
                for t in range(NT):
                    pool.indirect_dma_start(SLOTS, bass.IndirectOffsetOnAxis(ap=POI[:, t:t + 1], axis=0),
                                            IDI[:, t:t + 1], None).then_inc(scat, 16)
                pool.wait_ge(scat, b * (16 * NT) + 16 * NT)
                nc.gpsimd.sem_inc(idn, 1)

        @block.tensor
        def _(pe):
            pe.wait_ge(made, NMADE)
            pe.wait_ge(wload, 16 * (1 + NT))
            with pe.Fori(0, B) as b:
                pe.wait_ge(ch, b * CH + 5 + CH0)
                for t in range(NT):
                    if t % 2 == 0:
                        pe.wait_ge(xts, b * (NT // 2) + (t // 2 + 1))
                    for c in range(2):
                        at = 2 * P * (t % 2) + P * c
                        mm = nc.tensor.transpose(psT[0:CC, t // 2 % 2, at:at + P], XM[:, t, CC * c:CC * c + CC],
                                                 ident[:, :])
                    if t % 2 == 1:
                        mm.then_inc(xtp, 1)
                pe.wait_ge(xts, b * (NT // 2) + (NT // 2 + 2))
                for t in range(NT):
                    for c in range(2):
                        mm = nc.tensor.matmul(psL[:, E_N * t:E_N * t + E_N], XT[:, c, P * t:P * t + P], WGs[:, c, :],
                                              start=(c == 0), stop=(c == 1))
                mm.then_inc(lg, 1)
                pe.wait_ge(ch, b * CH + 11 + CH0)
                nc.tensor.matmul(psK[:, 0:NT * E_N], TRI[:, :], OH[:, :, :].rearrange("p t e -> p (t e)"),
                                 start=True, stop=False)
                for t in range(NT - 1):
                    nc.tensor.matmul(psK[:, E_N * (t + 1):NT * E_N].rearrange("p (t e) -> p t e", e=E_N), ONE[:, :],
                                     OH[:, t:t + 1, :].to_broadcast([P, NT - 1 - t, E_N]), start=False, stop=False)
                nc.tensor.matmul(psK[:, 0:NT * E_N].rearrange("p (t e) -> p t e", e=E_N), ONE[:, :],
                                 RUN[:, :].rearrange("p (o e) -> p o e", o=1).to_broadcast([P, NT, E_N]),
                                 start=False, stop=True).then_inc(rk, 1)
            pe.wait_ge(ch, B * CH + CH0)
            nc.tensor.matmul(psC[0:E_N, 0:1], RUN[:, :], ONE[:, 0:1], start=True, stop=True).then_inc(fin, 1)
            pe.wait_ge(fin, 5)
            nc.tensor.matmul(psK[:, 0:E_N], NTB[:, :], UPTO[:, :], start=True, stop=True).then_inc(fin, 1)
            pe.wait_ge(fin, 16)
            nc.tensor.transpose(psC[0:2, 0:P], TL[:, :], ident[:, :]).then_inc(fin, 1)

        @block.scalar
        def _(act):
            nc.scalar.sem_inc(xts, 2)
            with act.Fori(0, B) as b:
                for i in range(NT // 2):
                    act.wait_ge(xtp, b * (NT // 2) + (i + 1))
                    for t in range(2):
                        a = nc.scalar.copy(XT[:, :, P * (2 * i + t):P * (2 * i + t + 1)],
                                           psT[0:CC, i % 2, 2 * P * t:2 * P * t + 2 * P]
                                           .rearrange("p (c t) -> p c t", c=2))
                    a.then_inc(xts, 1)

        @block.vector
        def _(dve):
            nc.vector.sem_inc(x3, 1)
            nc.vector.sem_inc(ch, CH0)
            dve.wait_ge(wload, 16 * (1 + NT))
            dve.wait_ge(made, NMADE)
            with dve.Fori(0, B) as b:
                n = [0]

                def link(ins):
                    n[0] += 1
                    ins.then_inc(ch, 1)
                    dve.wait_ge(ch, b * CH + (n[0] + CH0))

                dve.wait_ge(load, b * 32 + 32)
                nc.vector.tensor_tensor(X[:, :, 0:C], X[:, :, 0:C], O[:, :, :], ALU.add).then_inc(x3, 1)
                dve.wait_ge(x3, b + 2)
                for t in range(NT):
                    ins = nc.vector.bn_stats(ST[:, t, :], X[:, t, 0:C])
                link(ins)
                nc.vector.sem_inc(gate, 1)
                for t in range(NT):
                    ins = nc.vector.bn_aggr(MV[:, t, :], ST[:, t, :])
                link(ins)
                link(nc.vector.tensor_copy(X[:, :, C:C + 1], MV[:, :, 0:1]))
                link(nc.vector.tensor_scalar(VE[:, :, :], MV[:, :, 1:2], EPS, None, ALU.add))
                dve.wait_ge(rsq, b + 1)
                for t in range(NT):
                    ins = nc.vector.tensor_scalar(XM[:, t, :], X[:, t, 0:C], X[:, t, C:C + 1], X[:, t, C + 1:C + 2],
                                                  ALU.subtract, ALU.mult)
                link(ins)
                dve.wait_ge(lg, b + 1)
                link(nc.vector.tensor_tensor(LG[:, :, :], psL[:, 0:NT * E_N].rearrange("p (t e) -> p t e", e=E_N),
                                             BGs[:, :, :], ALU.add))
                link(nc.vector.tensor_reduce(LM[:, :, :], LG[:, :, :], AX.X, ALU.max))
                link(nc.vector.tensor_tensor(EQ[:, :, :], LG[:, :, :], LM[:, :, :].to_broadcast([P, NT, E_N]),
                                             ALU.is_equal))
                link(nc.vector.tensor_tensor(EQ[:, :, :], EQ[:, :, :], DESC[:, :, :], ALU.mult))
                link(nc.vector.tensor_reduce(LM[:, :, :], EQ[:, :, :], AX.X, ALU.max))
                link(nc.vector.tensor_tensor(OH[:, :, :], DESC[:, :, :], LM[:, :, :].to_broadcast([P, NT, E_N]),
                                             ALU.is_equal))
                dve.wait_ge(rk, b + 1)
                link(nc.vector.tensor_tensor(PW[:, :, :], psK[:, 0:NT * E_N].rearrange("p (t e) -> p t e", e=E_N),
                                             EB[:, :, :], ALU.add))
                link(nc.vector.tensor_tensor(PW[:, :, :], PW[:, :, :], OH[:, :, :], ALU.mult))
                link(nc.vector.tensor_reduce(PO[:, :, :], PW[:, :, :], AX.X, ALU.add))
                dve.wait_ge(idn, b + 1)
                link(nc.vector.tensor_copy(POI[:, :], PO[:, :, 0]))
                link(nc.vector.tensor_copy(IDI[:, :], IDF[:, :]))
                link(nc.vector.tensor_reduce(OS[:, :], OH[:, :, :].rearrange("p t e -> p e t"), AX.X, ALU.add))
                link(nc.vector.tensor_tensor(RUN[:, :], RUN[:, :], OS[:, :], ALU.add))
                link(nc.vector.tensor_scalar(IDF[:, :], IDF[:, :], float(L), None, ALU.add))
                assert n[0] == CH

            def step(at, ins):
                ins.then_inc(fin, 1)
                dve.wait_ge(fin, at)

            dve.wait_ge(fin, 1)
            step(2, nc.vector.tensor_scalar(NTi[:, :], psC[0:E_N, 0:1], float(P - 1), None, ALU.add))
            step(3, nc.vector.tensor_scalar(NTi[:, :], NTi[:, :], 7, None, ALU.arith_shift_right))
            step(4, nc.vector.tensor_copy(NTe[:, :], NTi[:, :]))
            step(5, nc.vector.tensor_copy(NTB[:, :], NTe[:, :].to_broadcast([E_N, P])))
            dve.wait_ge(fin, 6)
            step(7, nc.vector.tensor_copy(END[:, :], psK[:, 0:E_N]))
            step(8, nc.vector.tensor_scalar(GE[:, :], END[:, :], JP[:, :], None, ALU.is_le))
            step(9, nc.vector.tensor_tensor(GEE[:, :], GE[:, :], END[:, :], ALU.mult))
            step(10, nc.vector.tensor_reduce(TL[:, 0:1], GE[:, :], AX.X, ALU.add))
            step(11, nc.vector.tensor_reduce(START[:, :], GEE[:, :], AX.X, ALU.max))
            step(12, nc.vector.tensor_tensor(START[:, :], JP[:, :], START[:, :], ALU.subtract))
            step(13, nc.vector.tensor_scalar(START[:, :], START[:, :], float(P), None, ALU.mult))
            step(14, nc.vector.tensor_scalar(BASE[:, :], TL[:, 0:1], float(CAP), None, ALU.mult))
            step(15, nc.vector.tensor_tensor(TL[:, 1:2], START[:, :], BASE[:, :], ALU.add))
            step(16, nc.vector.tensor_scalar(TL[:, 0:1], TL[:, 0:1], float(E_N - 1), None, ALU.min))
            dve.wait_ge(fin, 17)
            step(18, nc.vector.tensor_copy(TR[:, :], psC[0:2, 0:P]))


def experts(nc, name, X3, SLOTS, TILES, W1, B1, W2, B2, OUT):
    UN = 40
    NB = 8
    LAG = NB - 2
    assert NTILE % UN == 0 and UN % NB == 0
    with ExitStack() as ctx:
        def sb(n, shape, dt=F32):
            return ctx.enter_context(nc.sbuf_tensor(f"{name}_{n}", shape, dt))

        def ps(n, shape):
            return ctx.enter_context(nc.psum_tensor(f"{name}_{n}", shape, F32))

        def sem(n):
            return ctx.enter_context(nc.semaphore(f"{name}_{n}"))

        TLs = sb("tiles", [1, 2, P], I32)
        IXA = sb("slotsAll", [P, NTILE], I32)
        IX = sb("slots", [P, UN], I32)
        WA = sb("w1", [CC + 1, 2, E_N, C])
        WB = sb("w2", [CC + 1, 2, E_N, C])
        XG = sb("x", [P, NB, CM])
        XM = sb("xm", [P, 2, C])
        XT = sb("xmT", [CC + 1, 2, 2, P])
        H = sb("h", [P, 2, C])
        HT = sb("hT", [CC + 1, 2, 2, P])
        Y = sb("y", [P, NB, C])
        ident = sb("ident", [P, P])
        psX = ps("psX", [P, 2, 512])
        psH = ps("psH", [P, 2, 512])
        psG = ps("psG", [P, 2, 512])
        psY = ps("psY", [P, 2, 512])

        tl = sem("tl")
        wl = sem("wl")
        made = sem("made")
        ixa = [sem(f"ixa{i}") for i in range(2)]
        ix = sem("ix")
        got = [sem(f"got{i}") for i in range(NB)]
        put = [sem(f"put{i}") for i in range(NB)]
        free = sem("free")
        xm = sem("xm")
        xtp = sem("xtp")
        xts = sem("xts")
        hp = sem("hp")
        hs = sem("hs")
        htp = sem("htp")
        hts = sem("hts")
        yp = sem("yp")
        ys = sem("ys")
        gate = sem("gate")

        block = ctx.enter_context(nc.Block())

        def load_slots(eng, j0, j1, done):
            with eng.Fori(j0, j1) as j:
                first = eng.value_load(TLs[0:1, 1, bass.ds(j, 1)], min_val=0, max_val=LIST - P)
                with nc.allow_non_contiguous_dma(reason="a slot to each partition"):
                    eng.dma_start(IXA[:, bass.ds(j, 1)], SLOTS[bass.ds(first, P), :]).then_inc(done, 16)

        @block.sync
        def _(sp):
            sp.dma_start(TLs[:, :, :], TILES.rearrange("(o a) b -> o a b", o=1)).then_inc(tl, 16)
            for w, wt, bias in ((WA, W1, B1), (WB, W2, B2)):
                sp.dma_start(w[0:CC], wt.rearrange("(c p) e n -> p c e n", p=CC)).then_inc(wl, 16)
                sp.dma_start(w[CC:CC + 1, 1], bias.rearrange("(o e) n -> o e n", o=1)).then_inc(wl, 16)
            sp.wait_ge(tl, 16)
            load_slots(sp, 0, NTILE // 2, ixa[0])

        @block.gpsimd
        def _(pool):
            make_identity(nc, pool, ident, made)
            pool.wait_ge(made, 2)
            nc.gpsimd.memset(XT[CC:CC + 1], 1.0).then_inc(made, 1)
            pool.wait_ge(made, 3)
            nc.gpsimd.memset(HT[CC:CC + 1], 1.0).then_inc(made, 1)
            pool.wait_ge(made, 4)
            nc.gpsimd.memset(XG[:, :, :], 0.0).then_inc(made, 1)
            pool.wait_ge(made, 5)
            for half in ixa:
                pool.wait_ge(half, 16 * NTILE // 2)

            def put_back(i, k):
                q = k % NB
                pool.wait_ge(ys, i * UN + (k + 1 + 2))
                nc.gpsimd.sem_inc(gate, 1)
                pool.indirect_dma_start(OUT, bass.IndirectOffsetOnAxis(ap=IX[:, k:k + 1], axis=0), Y[:, q, :], None,
                                        bounds_check=T - 1, oob_is_err=False).then_inc(put[q], 16)

            with pool.Fori(0, NTILE // UN) as i:
                nc.gpsimd.tensor_copy(IX[:, :], IXA[:, bass.ds(i * UN, UN)]).then_inc(ix, 1)
                pool.wait_ge(ix, i + 1)
                nc.gpsimd.sem_inc(gate, 1)
                for k in range(UN):
                    q = k % NB
                    if k >= NB:
                        pool.wait_ge(put[q], i * (16 * UN // NB) + 16 * (k // NB))
                    nc.gpsimd.sem_inc(free, 1)
                    pool.indirect_dma_start(XG[:, q, :], None, X3, bass.IndirectOffsetOnAxis(ap=IX[:, k:k + 1], axis=0),
                                            bounds_check=T - 1, oob_is_err=False).then_inc(got[q], 16)
                    if k >= LAG:
                        put_back(i, k - LAG)
                for k in range(UN - LAG, UN):
                    put_back(i, k)
                for q in range(NB):
                    pool.wait_ge(put[q], i * (16 * UN // NB) + 16 * (UN // NB))
                nc.gpsimd.sem_inc(gate, 1)

        @block.tensor
        def _(pe):
            pe.wait_ge(made, 5)
            pe.wait_ge(tl, 16)
            pe.wait_ge(wl, 64)

            def turn(dst, src, done):
                for c in range(2):
                    mm = nc.tensor.transpose(dst[0:CC, P * c:P * c + P], src[:, CC * c:CC * c + CC], ident[:, :])
                mm.then_inc(done, 1)

            def layer(dst, xT, w, e, done):
                for c in range(2):
                    k = CC + c
                    mm = nc.tensor.matmul(dst[:, 0:C], xT[0:k, c, :], w[0:k, c, bass.ds(e, 1), :]
                                          .rearrange("p o n -> p (o n)"), start=(c == 0), stop=(c == 1))
                mm.then_inc(done, 1)

            with pe.Fori(0, NTILE // UN) as i:
                ex = [None] * UN
                for k in range(UN + 3):
                    n = i * UN
                    if k < UN:
                        pe.wait_ge(xm, n + (k + 1))
                        pe.wait_ge(xts, n + (k + 1))
                        turn(psX[:, k % 2, :], XM[:, k % 2, :], xtp)
                    if 1 <= k <= UN:
                        m = k - 1
                        ex[m] = pe.value_load(TLs[0:1, 0, bass.ds(n + m, 1)], min_val=0, max_val=E_N - 1)
                        pe.wait_ge(xts, n + (m + 1 + 2))
                        pe.wait_ge(hs, n + (m + 1))
                        layer(psH[:, m % 2, :], XT[:, m % 2], WA, ex[m], hp)
                    if 2 <= k <= UN + 1:
                        m = k - 2
                        pe.wait_ge(hs, n + (m + 1 + 2))
                        pe.wait_ge(hts, n + (m + 1))
                        turn(psG[:, m % 2, :], H[:, m % 2, :], htp)
                    if 3 <= k:
                        m = k - 3
                        pe.wait_ge(hts, n + (m + 1 + 2))
                        pe.wait_ge(ys, n + (m + 1))
                        layer(psY[:, m % 2, :], HT[:, m % 2], WB, ex[m], yp)

        @block.scalar
        def _(act):
            nc.scalar.sem_inc(xts, 2)
            nc.scalar.sem_inc(hs, 2)
            nc.scalar.sem_inc(hts, 2)
            act.wait_ge(tl, 16)
            load_slots(act, NTILE // 2, NTILE, ixa[1])
            act.wait_ge(made, 5)

            def to_sbuf(dst, src, done):
                nc.scalar.copy(dst[0:CC], src[0:CC, 0:2 * P].rearrange("p (c t) -> p c t", c=2)).then_inc(done, 1)

            with act.Fori(0, NTILE // UN) as i:
                n = i * UN
                for k in range(UN + 2):
                    if k < UN:
                        act.wait_ge(xtp, n + (k + 1 + 2))
                        act.wait_ge(hp, n + (k + 1))
                        to_sbuf(XT[:, k % 2], psX[:, k % 2, :], xts)
                    if 1 <= k <= UN:
                        m = k - 1
                        act.wait_ge(hp, n + (m + 1 + 2))
                        nc.scalar.activation(H[:, m % 2, :], psH[:, m % 2, 0:C], ACT.Gelu).then_inc(hs, 1)
                    if 2 <= k:
                        m = k - 2
                        act.wait_ge(htp, n + (m + 1))
                        act.wait_ge(yp, n + (m + 1))
                        to_sbuf(HT[:, m % 2], psG[:, m % 2, :], hts)

        @block.vector
        def _(dve):
            nc.vector.sem_inc(xtp, 2)
            nc.vector.sem_inc(hp, 2)
            nc.vector.sem_inc(yp, 2)
            nc.vector.sem_inc(ys, 2)
            with dve.Fori(0, NTILE // UN) as i:
                n = i * UN
                for k in range(UN + 4):
                    if k < UN:
                        q, p = k % NB, k % 2
                        dve.wait_ge(got[q], i * (16 * UN // NB) + 16 * (k // NB + 1))
                        dve.wait_ge(xtp, n + (k + 1))
                        nc.vector.tensor_scalar(XM[:, p, :], XG[:, q, 0:C], XG[:, q, C:C + 1], XG[:, q, C + 1:CM],
                                                ALU.subtract, ALU.mult).then_inc(xm, 1)
                    if k >= 4:
                        m = k - 4
                        dve.wait_ge(yp, n + (m + 1 + 2))
                        dve.wait_ge(free, n + (m + 1))
                        nc.vector.tensor_tensor(Y[:, m % NB, :], psY[:, m % 2, 0:C], XG[:, m % NB, 0:C], ALU.add)\
                            .then_inc(ys, 1)


def hybrid_block(nc, a, out):
    def dram(n, shape, dt=F32):
        return nc.dram_tensor(n, shape, dt, kind=DRAM_KIND).ap()

    QK1 = dram("qk1", (B, 2, 2 * C, L), F16)
    RL1 = dram("rel1", (STEPS, 2, 2, P, L), F16)
    VN1 = dram("v1", (STEPS, P, KT, GH, VW))
    O1 = dram("attn1", (T, C))
    X2 = dram("x2", (T, C))
    QK2 = dram("qk2", (B, 2, 2 * C, L), F16)
    VN2 = dram("v2", (STEPS, P, KT, GH, VW))
    O2 = dram("attn2", (T, C))
    X3 = dram("x3", (T, CM))
    SLOTS = dram("slots", (LIST, 1), I32)
    TILES = dram("tiles", (2, P), I32)
    const = {"group": a["group"], "sc": a["sc1"]}
    project(nc, "p1", True, a["xT"], {"wqk": a["c_wqk"], "bqk": a["c_bqk"], "wv": a["c_wv"], "bv": a["c_bv"],
                                      "relT": a["relT"]}, const, QK1, VN1, RL=RL1)
    attention(nc, "a1", True, 1.0, QK1, RL1, VN1, O1, a["onehot"])
    const = {"group": a["group"], "sc": a["sc2"]}
    project(nc, "p2", False, a["x"], {"wqk": a["a_wqk"], "bqk": a["a_bqk"], "wv": a["a_wv"], "bv": a["a_bv"],
                                      "proj_w": a["proj_w"], "proj_b": a["proj_b"]}, const, QK2, VN2, ON=O1, X2=X2)
    attention(nc, "a2", False, 1.0 / float(np.sqrt(C)), QK2, None, VN2, O2, a["onehot"])
    route(nc, "r", X2, O2, a["wg"], a["bg"], X3, SLOTS, TILES)
    experts(nc, "e", X3, SLOTS, TILES, a["w1"], a["b1"], a["w2"], a["b2"], out)


DRAM_KIND = "Internal"


def constants():
    t = np.arange(L)
    onehot = np.zeros((REL + 2, L), np.float16)
    onehot[t // WI, t] = 1
    onehot[HI + t % WI, t] = 1
    onehot[REL] = MAXSCALE
    c = np.arange(CC)
    n = C // GROUPS
    group = ((c[:, None] // n == c[None, :] // n) / n).astype(np.float32)
    rows = np.arange(NCH)[None, :] * P + np.arange(P)[:, None]
    sc1 = np.where(rows < C, 1.0, HD ** -0.5).astype(np.float32)
    return {"onehot": onehot, "group": group, "sc1": sc1, "sc2": np.ones((P, NCH), np.float32)}


def kernel(**inputs):
    import concourse.bacc as _bacc
    from concourse.bass_utils import run_bass_kernel_spmd as _run

    i = {k: np.asarray(v) for k, v in inputs.items()}
    x = i["x"].reshape(T, C)
    qkv_w, qkv_b = i["L0_conv_qkv_w"], i["L0_conv_qkv_b"]
    given = {
        "x": x, "xT": x.T,
        "c_wqk": qkv_w[:, :2 * C], "c_bqk": qkv_b[:2 * C], "c_wv": qkv_w[:, 2 * C:], "c_bv": qkv_b[2 * C:],
        "relT": np.stack([i["L0_conv_rel_pos_h"][::-1].T, i["L0_conv_rel_pos_w"][::-1].T]),
        "proj_w": i["L0_conv_proj_w"], "proj_b": i["L0_conv_proj_b"],
        "a_wqk": np.concatenate([i["L1_attn_Wq"], i["L1_attn_Wk"]], 1),
        "a_bqk": np.concatenate([i["L1_attn_bq"], i["L1_attn_bk"]]),
        "a_wv": i["L1_attn_Wv"], "a_bv": i["L1_attn_bv"],
        "wg": i["L1_ffn_Wg"].T, "bg": i["L1_ffn_bg"],
        "w1": i["L1_ffn_W1"].transpose(2, 0, 1), "b1": i["L1_ffn_b1"],
        "w2": i["L1_ffn_W2"].transpose(2, 0, 1), "b2": i["L1_ffn_b2"],
        **constants(),
    }
    nc = _bacc.Bacc("TRN2", target_bir_lowering=False, num_devices=1)
    arrays, aps = {}, {}
    for name, a in given.items():
        a = np.ascontiguousarray(a)
        arrays[f"in_{name}"] = a
        aps[name] = nc.dram_tensor(f"in_{name}", a.shape, mybir.dt.from_np(a.dtype), kind="ExternalInput").ap()
    out = nc.dram_tensor("out_0", (T, C), F32, kind="ExternalOutput").ap()
    hybrid_block(nc, aps, out)
    r = _run(nc, [arrays], core_ids=[0])
    return r.results[0]["out_0"].reshape(B, HI, WI, C)
```

```python
from contextlib import ExitStack

import concourse.bass as bass
import numpy as np
from concourse import mybir

F32 = mybir.dt.float32
F16 = mybir.dt.float16
I32 = mybir.dt.int32
ALU = mybir.AluOpType
ACT = mybir.ActivationFunctionType
AX = mybir.AxisListType

P = 128
B, HI, WI, C = 8, 32, 32, 192
L = HI * WI
T = B * L
NH, HD = 12, 16
GH = 4
NG = NH // GH
STEPS = B * NG
CC = C // 2
KT = L // P
QH = L // 512
VW = 2 * HD
REL = HI + WI
PAIR = 2 * L
ROUNDS = T // PAIR
NCH = 3
GROUPS = 32
MAXSCALE = 64.0
E_N = 16


def make_identity(nc, pool, ident, done):
    nc.gpsimd.memset(ident[:, :], 0.0).then_inc(done, 1)
    pool.wait_ge(done, 1)
    nc.gpsimd.affine_select(out=ident[:, :], in_=ident[:, :], compare_op=ALU.not_equal, fill=1.0,
                            base=0, pattern=[[-1, P]], channel_multiplier=1).then_inc(done, 1)


def attention(nc, name, rel, scale, QK, RL, VN, ON, onehot_dram):
    KQ = (3 if rel else 4) * HD
    R = KQ + (REL if rel else 1)
    NBUF = 3
    BLK = QH * KT
    UNITS = GH * KT
    HALVES = 2 * UNITS
    MAXBLK = BLK - 3
    with ExitStack() as ctx:
        def sb(n, shape, dt):
            return ctx.enter_context(nc.sbuf_tensor(f"{name}_{n}", shape, dt))

        def sem(n):
            return ctx.enter_context(nc.semaphore(f"{name}_{n}"))

        A = [sb(f"qrows{i}", [R + 1, GH, L], F16) for i in range(NBUF)]
        K = [sb(f"krows{i}", [R + 1, GH, L], F16) for i in range(NBUF)]
        V = [sb(f"v{i}", [P, KT, GH, VW], F32) for i in range(NBUF)]
        if rel:
            RLO = [sb(f"rello{i}", [P, GH // 2, L], F16) for i in range(NBUF)]
            E = sb("onehot", [P, L], F16)
        PT = sb("probs", [P, 2, GH, 512], F32)
        MX = [sb(f"halfmax{i}", [P, UNITS, 2], F32) for i in range(NBUF)]
        MC = sb("rowmax", [P, UNITS], F32)
        MT = sb("rowmaxT", [UNITS, P], F16)
        OT = sb("outT", [P, QH, 512], F32)
        RC = sb("recip", [P, 4 * GH, 1], F32)
        OS = sb("out", [P, QH, 4 * GH, HD], F32)
        ident = sb("ident", [P, P], F32)
        psS = ctx.enter_context(nc.psum_tensor(f"{name}_psS", [P, 4, 512], F32))
        psR = ctx.enter_context(nc.psum_tensor(f"{name}_psR", [P, 3, 512], F32))
        psO = ctx.enter_context(nc.psum_tensor(f"{name}_psO", [P, 512], F32))

        const_done = sem("const_done")
        const_dma = sem("const_dma")
        loaded = [sem(f"loaded{i}") for i in range(NBUF)]
        mrow = sem("mrow")
        scores = sem("scores")
        exped = sem("exped")
        pvdone = sem("pvdone")
        ring_full = sem("ring_full")
        ring_free = sem("ring_free")
        maxed = sem("maxed")
        otc = sem("otc")
        recips = sem("recips")
        stored = [sem(f"stored{i}") for i in range(QH)]

        NL = 8 + 1 if not rel else 6 + 1 + 2 + 4
        LB = 16 * NL
        PER_BLK = HALVES // BLK
        EARLY = PER_BLK * (BLK - MAXBLK)

        def jobs_of(g, last):
            after = [[] for _ in range(BLK + 1)]
            for blk in range(BLK):
                offset, u = (1, EARLY + PER_BLK * blk) if blk < MAXBLK else (2, PER_BLK * (blk - MAXBLK))
                if not (last and g + offset >= NG):
                    after[blk] += [("max", u + i, offset) for i in range(PER_BLK)]
            if not (last and g == NG - 1):
                after[MAXBLK].insert(2, ("rows",))
            after[KT + 2].append(("back", 0, 0))
            if g > 0:
                after[2].append(("back", -1, 1))
            if g == NG - 1:
                after[BLK].append(("back", 0, 1))
            return after

        PROLOGUE = HALVES + 1 + EARLY
        FIRST = [("max", u, 0) for u in range(HALVES)] + [("rows",)] + [("max", u, 1) for u in range(EARLY)]

        def number(last):
            at, out = 0, []
            for g in range(NG):
                after = []
                for js in jobs_of(g, last):
                    after.append([(at + n, j) for n, j in enumerate(js)])
                    at += len(js)
                out.append(after)
            return out, at

        JOBS, PER_B = number(False)
        JOBS_LAST, _ = number(True)
        assert PER_B % 3 == 0

        def back_number(jobs, g, qh):
            for gg in range(NG):
                for js in jobs[gg]:
                    for n, j in js:
                        if j[0] == "back" and gg + j[1] == g and j[2] == qh:
                            return n
            raise ValueError

        def rows_number(jobs, g):
            return next(n for n, j in jobs[g][MAXBLK] if j[0] == "rows")

        block = ctx.enter_context(nc.Block())

        @block.gpsimd
        def _(pool):
            make_identity(nc, pool, ident, const_done)

        @block.sync
        def _(sp):
            def load(b, g, buf):
                def rows(c0, part):
                    c = c0 + HD * GH * g
                    return QK[b, part, c:c + HD * GH, :].rearrange("(h d) t -> d h t", h=GH)

                s = b * NG + g
                for n, (pq, pk) in enumerate(((0, 0), (0, 1), (1, 0), (1, 1))[:KQ // HD]):
                    sp.dma_start(A[buf][HD * n:HD * (n + 1), :, :], rows(0, pq)).then_inc(loaded[buf], 16)
                    sp.dma_start(K[buf][HD * n:HD * (n + 1), :, :], rows(C, pk)).then_inc(loaded[buf], 16)
                sp.dma_start(V[buf][:, :, :, :], VN[s]).then_inc(loaded[buf], 16)
                if rel:
                    for hw in range(2):
                        src = RL[s, 0, hw].rearrange("(k h) t -> k h t", h=GH)
                        sp.dma_start(A[buf][KQ + 32 * hw:KQ + 32 * hw + 32, :, :], src).then_inc(loaded[buf], 16)
                        for r in range(2):
                            src = RL[s, 1, hw].rearrange("(k a r) t -> r k a t", r=2, a=2)[r]
                            sp.dma_start(RLO[buf][64 * r + 32 * hw:64 * r + 32 * hw + 32, :, :], src)\
                              .then_inc(loaded[buf], 16)

            def row_of_maxima(buf, free):
                sp.wait_ge(ring_free, free)
                for h in range(GH):
                    sp.dma_start(A[buf][R:R + 1, h, :].rearrange("o (t p) -> o t p", p=P),
                                 MT[KT * h:KT * h + KT, :]).then_inc(mrow, 16)

            def store(b, g, qh, jobs):
                sp.wait_ge(ring_free, PROLOGUE + b * PER_B + back_number(jobs, g, qh) + 4)
                dst = ON[bass.ds(b * L + qh * 512, 512), GH * HD * g:GH * HD * (g + 1)]
                sp.dma_start(dst.rearrange("(t p) c -> p t c", p=P),
                             OS[:, qh, :, :].rearrange("p (t h) d -> p t (h d)", t=4)).then_inc(stored[qh], 16)

            for qh in range(QH):
                nc.sync.sem_inc(stored[qh], 16)
            for i in range(NBUF):
                for h in range(GH):
                    if rel:
                        sp.dma_start(K[i][KQ:R, h, :], onehot_dram[0:REL, :]).then_inc(const_dma, 16)
                    else:
                        sp.dma_start(K[i][KQ:R, h, :], onehot_dram[REL + 1:REL + 2, :]).then_inc(const_dma, 16)
                        sp.dma_start(A[i][KQ:R, h, :], onehot_dram[REL + 1:REL + 2, :]).then_inc(const_dma, 16)
                    sp.dma_start(K[i][R:R + 1, h, :], onehot_dram[REL:REL + 1, :]).then_inc(const_dma, 16)
            if rel:
                for r in range(2):
                    sp.dma_start(E[64 * r:64 * r + 64, :], onehot_dram[0:REL, :]).then_inc(const_dma, 16)
            load(0, 0, 0)
            load(0, 1, 1)
            row_of_maxima(0, HALVES + 4)

            def step(b, g, jobs, last):
                if not (last and g > 0):
                    sp.wait_ge(pvdone, b * (NG * BLK) + g * BLK + 2)
                    load(b if g == 0 else b + 1, 2 if g == 0 else g - 1, (g + 2) % NBUF)
                if g > 0:
                    store(b, g - 1, 1, jobs)
                store(b, g, 0, jobs)
                if not (last and g == NG - 1):
                    row_of_maxima((g + 1) % NBUF, PROLOGUE + b * PER_B + rows_number(jobs, g) + 4)
                if g == NG - 1:
                    store(b, g, 1, jobs)

            with sp.Fori(0, B - 1) as b:
                for g in range(NG):
                    step(b, g, JOBS, False)
            for g in range(NG):
                step(B - 1, g, JOBS_LAST, True)
            for qh in range(QH):
                sp.wait_ge(stored[qh], 16 * STEPS + 16)

        @block.tensor
        def _(pe):
            def job(jn, j, base, slot, g, halves, rows):
                pe.wait_ge(ring_free, base + jn + 1)
                if j[0] == "max":
                    u, half = j[1] // 2, j[1] % 2
                    h, qt, buf = u // KT, u % KT, (g + j[2]) % NBUF
                    mm = nc.tensor.matmul(psR[:, slot, :], A[buf][0:R, h, P * qt:P * qt + P],
                                          K[buf][0:R, h, 512 * half:512 * half + 512], start=True, stop=True)
                elif j[0] == "rows":
                    pe.wait_ge(maxed, rows + 1)
                    mm = nc.tensor.transpose(psR[0:UNITS, slot, 0:P], MC[:, :], ident[:, :])
                else:
                    pe.wait_ge(otc, halves + QH * j[1] + j[2] + 2)
                    for qt in range(4):
                        mm = nc.tensor.transpose(psR[:, slot, P * qt:P * qt + P],
                                                 OT[:, j[2], P * qt:P * qt + P], ident[:, :])
                mm.then_inc(ring_full, 1)

            def scores_pair(buf, kt, qh, pair, n, pairs):
                pe.wait_ge(exped, pairs + n + 1)
                for j in range(2):
                    h = 2 * pair + j
                    mm = nc.tensor.matmul(psS[:, (2 * n + j) % 4, :], K[buf][0:R + 1, h, P * kt:P * kt + P],
                                          A[buf][0:R + 1, h, 512 * qh:512 * qh + 512], start=True, stop=not rel)
                if rel:
                    for j in range(2):
                        mm = nc.tensor.matmul(psS[:, (2 * n + j) % 4, :],
                                              E[64 * j:64 * j + 64, P * kt:P * kt + P],
                                              RLO[buf][64 * j:64 * j + 64, pair, 512 * qh:512 * qh + 512],
                                              start=False, stop=True)
                mm.then_inc(scores, 1)

            def pv(buf, blk, blks, halves):
                kt, qh = blk % KT, blk // KT
                pe.wait_ge(exped, 2 * (blks + blk + 1) + 2)
                if kt == 0:
                    pe.wait_ge(otc, halves + qh + 1)
                for h in range(GH):
                    mm = nc.tensor.matmul(psO[32 * h:32 * h + 32, :], V[buf][:, kt, h, :], PT[:, blk % 2, h, :],
                                          start=(kt == 0), stop=(kt == KT - 1))
                mm.then_inc(pvdone, 1)

            def step(b, g, jobs, last):
                s = b * NG + g
                blks, halves, base = s * BLK, s * QH, PROLOGUE + b * PER_B
                pe.wait_ge(mrow, s * (16 * GH) + 16 * GH)
                for blk in range(BLK):
                    if blk == MAXBLK and not (last and g + 2 >= NG):
                        pe.wait_ge(loaded[(g + 2) % NBUF], b * LB + ((g + 2) // NG + 1) * LB)
                    js = jobs[g][blk]
                    cuts = [0, len(js) // 2, max(len(js) - 1, len(js) // 2), len(js)]
                    for part in range(3):
                        if part < 2:
                            scores_pair(g, blk % KT, blk // KT, part, 2 * blk + part, 2 * blks)
                        elif blk >= 1:
                            pv(g, blk - 1, blks, halves)
                        elif g > 0:
                            pv(g - 1, BLK - 1, blks - BLK, halves - QH)
                        for jn, j in js[cuts[part]:cuts[part + 1]]:
                            job(jn, j, base, (PROLOGUE + jn) % 3, g, halves, s + 1)
                if g == NG - 1:
                    pv(g, BLK - 1, blks, halves)
                    for jn, j in jobs[g][BLK]:
                        job(jn, j, base, (PROLOGUE + jn) % 3, g, halves, s + 1)

            pe.wait_ge(const_done, 2)
            pe.wait_ge(const_dma, 16 * (NBUF * GH * (2 if rel else 3) + (2 if rel else 0)))
            pe.wait_ge(loaded[0], LB)
            for n, j in enumerate(FIRST):
                if n == HALVES + 1:
                    pe.wait_ge(loaded[1], LB)
                job(n, j, 0, n % 3, 0, 0, 0)
            with pe.Fori(0, B - 1) as b:
                for g in range(NG):
                    step(b, g, JOBS, False)
            for g in range(NG):
                step(B - 1, g, JOBS_LAST, True)

        @block.scalar
        def _(act):
            nc.scalar.sem_inc(exped, 2)
            nc.scalar.sem_inc(otc, 1)

            def copy_out(b, g, qh, jobs):
                act.wait_ge(pvdone, b * (NG * BLK) + g * BLK + KT * (qh + 1) + 2)
                before = back_number(JOBS, NG - 1, qh) - PER_B if g == 0 else back_number(jobs, g - 1, qh)
                act.wait_ge(ring_free, b * PER_B + (PROLOGUE + before + 4))
                nc.scalar.copy(OT[:, qh, :], psO[:, :]).then_inc(otc, 1)

            def step(b, g, jobs):
                s = b * NG + g
                for n in range(2 * BLK):
                    blk, pair = n // 2, n % 2
                    act.wait_ge(scores, s * (2 * BLK) + n + 1)
                    act.wait_ge(pvdone, s * BLK + blk + 1)
                    b0 = 2 * n % 4
                    nc.scalar.activation(PT[:, blk % 2, 2 * pair:2 * pair + 2, :], psS[:, b0:b0 + 2, :], ACT.Exp,
                                         scale=scale).then_inc(exped, 1)
                    if n == 1 and g > 0:
                        copy_out(b, g - 1, 1, jobs)
                    if n == 2 * KT + 1:
                        copy_out(b, g, 0, jobs)
                if g == NG - 1:
                    copy_out(b, g, 1, jobs)

            with act.Fori(0, B - 1) as b:
                for g in range(NG):
                    step(b, g, JOBS)
            for g in range(NG):
                step(B - 1, g, JOBS_LAST)

        @block.vector
        def _(dve):
            nc.vector.sem_inc(pvdone, 2)
            nc.vector.sem_inc(ring_free, 3)

            def job(jn, j, base, slot, g, steps):
                dve.wait_ge(ring_full, base + jn + 1)
                if j[0] == "max":
                    mx = MX[(g + j[2]) % NBUF]
                    nc.vector.tensor_reduce(mx[:, j[1] // 2, j[1] % 2:j[1] % 2 + 1], psR[:, slot, :], AX.X, ALU.max)\
                        .then_inc(ring_free, 1)
                    if j[1] == HALVES - 1:
                        dve.wait_ge(ring_free, base + jn + 4)
                        nc.vector.tensor_tensor(MC[:, :], mx[:, :, 0], mx[:, :, 1], ALU.max).then_inc(maxed, 1)
                elif j[0] == "rows":
                    if steps is not None:
                        dve.wait_ge(mrow, steps * (16 * GH) + 16 * GH)
                    nc.vector.tensor_scalar(MT[:, :], psR[0:UNITS, slot, 0:P], -1.0 / MAXSCALE, None, ALU.mult)\
                        .then_inc(ring_free, 1)
                else:
                    qh, half = j[2], steps * QH + j[1] * QH + j[2]
                    o = psR[:, slot, :].rearrange("p (x v) -> p x v", v=VW)
                    dve.wait_ge(ring_free, base + jn + 3)
                    nc.vector.reciprocal(RC[:, :, :], o[:, :, HD:HD + 1]).then_inc(recips, 1)
                    dve.wait_ge(recips, half + 1)
                    dve.wait_ge(stored[qh], steps * 16 + (16 * j[1] + 16))
                    nc.vector.tensor_tensor(OS[:, qh, :, :], o[:, :, 0:HD], RC[:, :, :].to_broadcast([P, 4 * GH, HD]),
                                            ALU.mult).then_inc(ring_free, 1)

            for n, j in enumerate(FIRST):
                job(n, j, 0, n % 3, 0, None)

            def step(b, g, jobs):
                for js in jobs[g]:
                    for jn, j in js:
                        job(jn, j, PROLOGUE + b * PER_B, (PROLOGUE + jn) % 3, g, b * NG + g)

            with dve.Fori(0, B - 1) as b:
                for g in range(NG):
                    step(b, g, JOBS)
            for g in range(NG):
                step(B - 1, g, JOBS_LAST)


def project(nc, name, first, IN, W, CONST, QK, VN, RL=None, ON=None, X2=None):
    NT = PAIR // P
    assert NCH == 3
    RX = 8
    EPS = 1e-5
    with ExitStack() as ctx:
        def sb(n, shape, dt=F32):
            return ctx.enter_context(nc.sbuf_tensor(f"{name}_{n}", shape, dt))

        def ps(n, shape):
            return ctx.enter_context(nc.psum_tensor(f"{name}_{n}", shape, F32))

        def sem(n):
            return ctx.enter_context(nc.semaphore(f"{name}_{n}"))

        XN = sb("xnT", [CC, 2, PAIR])
        QF = sb("qk", [P, NCH, PAIR])
        HL = [sb(f"half{i}", [P, NCH, PAIR], F16) for i in range(2)]
        VT = sb("v", [P, NT, NH, VW])
        WQK = sb("wqk", [CC, 2, 2 * C])
        WV = sb("wv", [CC, 2, C])
        BQK = sb("bqk", [P, NCH])
        BV2 = sb("bv", [P, 2 * C])
        SC = sb("sc", [P, NCH])
        psQ = ps("psQ", [P, 2, 512])
        psV = ps("psV", [P, 2, 512])
        psR = ps("psR", [P, 4, 512])
        PROJ = [psV[:, 0, :], psV[:, 1, :], psR[:, 0, :], psR[:, 1, :]]

        wload = sem("wload")
        preset = sem("preset")
        xload = sem("xload")
        xnorm = sem("xnorm")
        qps = sem("qps")
        qf = sem("qf")
        vps = sem("vps")
        vt = sem("vt")
        hi = sem("hi")
        lo = sem("lo")
        qkst = sem("qkst")
        vst = sem("vst")
        rsq = sem("rsq")
        gate = sem("gate")
        if first:
            X = sb("xT", [CC, 2, PAIR])
            G = sb("groupmean", [CC, CC])
            ST = sb("stats", [CC, 4, 2, 6])
            MV = sb("meanvar", [CC, 4, 2])
            D = sb("between", [CC, 4])
            D2 = sb("spread", [CC, 4])
            GM = sb("gmean", [CC, 4])
            VE = sb("variance", [CC, 4])
            HALF = sb("half", [CC, 4])
            RS = sb("rstd", [CC, 4])
            RT = sb("relT", [P, 2, 2 * HI - 1, GH])
            RTS = [sb(f"relThalf{i}", [P, 2, 2 * HI - 1, GH], F16) for i in range(2)]
            split = sem("split")
            RH = [[sb(f"rel{g}_{i}", [P, 2, PAIR], F16) for i in range(2)] for g in range(NG)]
            dchain = sem("dchain")
            DC = 7
            gps = sem("gps")
            rps = sem("rps")
            rhi = sem("rhi")
            rlo = sem("rlo")
            rst = sem("rst")
            NR = NG * 2 * (HI // RX)
        else:
            O = sb("attn", [P, NT, C])
            X = sb("x", [P, NT, C])
            OTs = sb("attnT", [CC, 2, 2, P])
            XM = sb("xm", [P, NT, C])
            WP = sb("wproj", [CC, 2, C])
            BP = sb("bproj", [P, C])
            ST = sb("stats", [P, NT, 6])
            MV = sb("meanvar", [P, NT, 2])
            VE = sb("variance", [P, NT])
            HALF = sb("half", [P, NT])
            RS = sb("rstd", [P, NT])
            ident = sb("ident", [P, P])
            made = sem("made")
            oload = sem("oload")
            xb = sem("xb")
            otp = sem("otp")
            ots = sem("ots")
            pps = sem("pps")
            x2 = sem("x2")
            st = sem("st")
            xm = sem("xm")
            xtp = sem("xtp")
            x2st = sem("x2st")
        LAG = 12
        PIECES = 4 if first else NT
        NW = 16 * (6 + (1 + 2 * GH * 2 if first else 2))

        def rel_views(g, half, hw, x0, bank):
            src = psR[:, bank, :].rearrange("p (b x y) -> p b x y", b=2, x=RX)
            dst = RH[g][half][:, hw, :].rearrange("p (b h w) -> p b h w", b=2, h=HI)
            if hw == 0:
                return [dst[:, b, x0:x0 + RX, :] for b in range(2)], [src[:, b] for b in range(2)]
            return ([dst[:, b, :, x0:x0 + RX] for b in range(2)],
                    [src[:, b].rearrange("p x y -> p y x") for b in range(2)])

        block = ctx.enter_context(nc.Block())

        @block.sync
        def _(sp):
            for dst, src in ((WQK, W["wqk"].rearrange("(c p) n -> p c n", p=CC)),
                             (WV, W["wv"].rearrange("(c p) n -> p c n", p=CC)),
                             (SC, CONST["sc"])):
                sp.dma_start(dst[:], src).then_inc(wload, 16)
            with nc.allow_non_contiguous_dma(reason="biases, once"):
                sp.dma_start(BQK[:, :], W["bqk"].rearrange("(m p) -> p m", p=P)).then_inc(wload, 16)
            for t in range(2):
                sp.dma_start(BV2[:, C * t:C * t + C], W["bv"].rearrange("(o n) -> o n", o=1).to_broadcast([P, C]))\
                  .then_inc(wload, 16)
            if first:
                sp.dma_start(G[:, :], CONST["group"]).then_inc(wload, 16)
                sp.wait_ge(preset, 3)
                for r in range(2):
                    for h in range(GH):
                        for hw in range(2):
                            row = 64 * r + HD * h
                            with nc.allow_non_contiguous_dma(reason="a small table, once"):
                                sp.dma_start(RT[row:row + HD, hw, :, h], W["relT"][hw]).then_inc(wload, 16)
            else:
                sp.dma_start(WP[:], W["proj_w"].rearrange("(c p) n -> p c n", p=CC)).then_inc(wload, 16)
                sp.dma_start(BP[:, :], W["proj_b"].rearrange("(o n) -> o n", o=1).to_broadcast([P, C]))\
                  .then_inc(wload, 16)

            nc.sync.sem_inc(qkst, 16)
            nc.sync.sem_inc(vst, 16)
            nc.sync.sem_inc(rst if first else x2st, 16)
            def store_half(j, m, half):
                sp.wait_ge((hi, lo)[half], j * NCH + m + 1 + half)
                nc.sync.sem_inc(gate, 1)
                dst = QK[bass.ds(2 * j, 2), half, P * m:P * m + P, :].rearrange("b c t -> c b t")
                sp.dma_start(dst, HL[half][:, m, :].rearrange("p (b t) -> p b t", b=2)).then_inc(qkst, 16)

            with sp.Fori(0, ROUNDS) as j:
                if not first:
                    for q in range(4):
                        sp.wait_ge(x2, j * NT + 4 * (q + 1) + 4)
                        nc.sync.sem_inc(gate, 1)
                        dst = X2[bass.ds(j * PAIR + q * 512, 512), :].rearrange("(t p) c -> p t c", p=P)
                        sp.dma_start(dst, X[:, 4 * q:4 * q + 4, :]).then_inc(x2st, 16)
                for m, half in ((0, 0), (0, 1), (1, 0), (1, 1), (2, 0)):
                    store_half(j, m, half)
                sp.wait_ge(vt, j * (NT // 2) + NT // 2 + 2)
                nc.sync.sem_inc(gate, 1)
                for b in range(2):
                    for g in range(NG):
                        sp.dma_start(VN[j * (2 * NG) + (b * NG + g)],
                                     VT[:, b * KT:b * KT + KT, GH * g:GH * g + GH, :]).then_inc(vst, 16)
                if first:
                    for g in range(NG):
                        sp.wait_ge(rlo, j * NR + (NR // NG) * (g + 1) + 4)
                        nc.sync.sem_inc(gate, 1)
                        for half in range(2):
                            for b in range(2):
                                dst = RL[j * (2 * NG) + (b * NG + g), half].rearrange("w c t -> c w t")
                                sp.dma_start(dst, RH[g][half][:, :, b * L:b * L + L]).then_inc(rst, 16)
                        if g == NG // 2:
                            store_half(j, NCH - 1, 1)
                else:
                    store_half(j, NCH - 1, 1)
            sp.wait_ge(qkst, ROUNDS * 96 + 16)
            sp.wait_ge(vst, ROUNDS * 96 + 16)
            if first:
                sp.wait_ge(rst, ROUNDS * 192 + 16)
            else:
                sp.wait_ge(x2st, ROUNDS * 64 + 16)

        @block.gpsimd
        def _(pool):
            nc.gpsimd.memset(HALF[:, :], -0.5).then_inc(preset, 1)
            if first:
                nc.gpsimd.memset(RT[:, :, :, :], 0.0).then_inc(preset, 1)
            else:
                make_identity(nc, pool, ident, made)
            pool.wait_ge(wload, NW)
            pool.wait_ge(preset, 3 if first else 2)
            with pool.Fori(0, ROUNDS) as j:
                if first:
                    pool.wait_ge(xnorm, j * PIECES + 1)
                    nc.gpsimd.sem_inc(gate, 1)
                    src = IN[:, bass.ds(j * PAIR, PAIR)].rearrange("(c p) t -> p c t", p=CC)
                    pool.dma_start(X[:, :, :], src).then_inc(xload, 16)
                    pool.wait_ge(dchain, j * DC + DC)
                    nc.gpsimd.tensor_tensor(RS[:, :], VE[:, :], HALF[:, :], ALU.pow).then_inc(rsq, 1)
                else:
                    pool.wait_ge(x2st, j * 64 + 16)
                    pool.wait_ge(xnorm, j * PIECES + 1)
                    nc.gpsimd.sem_inc(gate, 1)
                    for dst, src, s in ((O, ON, oload), (X, IN, xload)):
                        pool.dma_start(dst[:, :, :], src[bass.ds(j * PAIR, PAIR), :]
                                       .rearrange("(t p) c -> p t c", p=P)).then_inc(s, 16)
                    pool.wait_ge(xload, j * 16 + 16)
                    nc.gpsimd.tensor_tensor(X[:, :, :], X[:, :, :], BP[:, :].rearrange("p (o c) -> p o c", o=1)
                                            .to_broadcast([P, NT, C]), ALU.add).then_inc(xb, 1)
                    for q in range(NT // 4):
                        pool.wait_ge(st, j * (3 * NT // 4) + (3 * q + 3))
                        nc.gpsimd.tensor_tensor(RS[:, 4 * q:4 * q + 4], VE[:, 4 * q:4 * q + 4],
                                                HALF[:, 4 * q:4 * q + 4], ALU.pow).then_inc(rsq, 1)

        @block.tensor
        def _(pe):
            pe.wait_ge(wload, NW)
            if first:
                pe.wait_ge(split, 2)
            else:
                pe.wait_ge(made, 2)

            def group_mean(n, j, src):
                pe.wait_ge(dchain, j * DC + (2, 6)[n])
                nc.tensor.matmul(psR[0:CC, n, 0:4], G[:, :], src, start=True, stop=True).then_inc(gps, 1)

            def turn_attn(i, j):
                if i == 0:
                    pe.wait_ge(oload, j * 16 + 16)
                    pe.wait_ge(qf, j * (4 * NCH) + 2)
                    pe.wait_ge(vt, j * (NT // 2) + 2)
                pe.wait_ge(ots, j * NT + i + 1)
                for c in range(2):
                    mm = nc.tensor.transpose(psQ[0:CC, i % 2, P * c:P * c + P], O[:, i, CC * c:CC * c + CC], ident[:, :])
                mm.then_inc(otp, 1)

            def proj(i, j):
                pe.wait_ge(ots, j * NT + i + 3)
                pe.wait_ge(x2, j * NT + i + 1)
                for c in range(2):
                    mm = nc.tensor.matmul(PROJ[i % 4][:, 0:C], OTs[:, i % 2, c, :], WP[:, c, :], start=(c == 0), stop=(c == 1))
                mm.then_inc(pps, 1)

            def turn_x(i, j):
                pe.wait_ge(xm, j * NT + i + 1)
                if i >= 2:
                    pe.wait_ge(xnorm, j * NT + i)
                for c in range(2):
                    mm = nc.tensor.transpose(psR[0:CC, 2 + i % 2, P * c:P * c + P], XM[:, i, CC * c:CC * c + CC],
                                             ident[:, :])
                mm.then_inc(xtp, 1)

            def round_of(j, last):
                ahead = first and not last
                if not first:
                    for i in range(NT + LAG):
                        if i < NT:
                            turn_attn(i, j)
                        if 1 <= i <= NT:
                            proj(i - 1, j)
                        if i >= LAG:
                            turn_x(i - LAG, j)
                if not first:
                    pe.wait_ge(xnorm, j * PIECES + PIECES + 1)
                n = 0
                for m in range(NCH):
                    for q in range(PAIR // 512):
                        if first and m == 0 and q % 2 == 0:
                            pe.wait_ge(xnorm, j * PIECES + (q + 3))
                        pe.wait_ge(qf, j * (4 * NCH) + (n + 1))
                        for c in range(2):
                            mm = nc.tensor.matmul(psQ[:, n % 2, :], WQK[:, c, P * m:P * m + P],
                                                  XN[:, c, 512 * q:512 * q + 512], start=(c == 0), stop=(c == 1))
                        mm.then_inc(qps, 1)
                        n += 1
                if ahead:
                    pe.wait_ge(rlo, j * NR + 4)
                    group_mean(0, j + 1, MV[:, :, 0])
                for t in range(NT):
                    if ahead and t == 4:
                        group_mean(1, j + 1, D2[:, :])
                    if t % 2 == 0:
                        pe.wait_ge(vt, j * (NT // 2) + (t // 2 + 1))
                    for c in range(2):
                        mm = nc.tensor.matmul(psV[:, t // 2 % 2, C * (t % 2):C * (t % 2) + C],
                                              XN[:, c, P * t:P * t + P], WV[:, c, :], start=(c == 0), stop=(c == 1))
                    if t % 2 == 1:
                        mm.then_inc(vps, 1)
                if ahead:
                    pe.wait_ge(dchain, (j + 1) * DC + DC)
                if first:
                    n = 0
                    for g in range(NG):
                        r, m = 64 * (g % 2), g // 2
                        pe.wait_ge(hi, j * NCH + m + 1)
                        pe.wait_ge(lo, j * NCH + m + 2)
                        q = [x[r:r + 64, m, :].rearrange("p (b h w) -> p b h w", b=2, h=HI) for x in HL]
                        for hw in range(2):
                            for x0 in range(0, HI, RX):
                                pe.wait_ge(rlo, j * NR + (n + 1))
                                o = psR[:, n % 4, :].rearrange("p (b x y) -> p b x y", b=2, x=RX)
                                for x in range(RX):
                                    xx = x0 + x
                                    for i, (part, of) in enumerate(((0, 0), (0, 1), (1, 0))):
                                        table = RTS[part][r:r + 64, hw, HI - 1 - xx:2 * HI - 1 - xx, :]
                                        mm = nc.tensor.matmul(o[:, :, x, :], table.rearrange("p k h -> p (k h)"),
                                                              q[of][:, :, xx, :] if hw == 0 else q[of][:, :, :, xx],
                                                              start=(i == 0), stop=(i == 2))
                                mm.then_inc(rps, 1)
                                n += 1

            if first:
                group_mean(0, 0, MV[:, :, 0])
                group_mean(1, 0, D2[:, :])
            with pe.Fori(0, ROUNDS - 1) as j:
                round_of(j, False)
            round_of(ROUNDS - 1, True)

        @block.scalar
        def _(act):
            nc.scalar.sem_inc(qf, 2)
            act.wait_ge(wload, NW)
            if first:
                nc.scalar.copy(RTS[0][:, :, :, :], RT[:, :, :, :]).then_inc(split, 1)
            if not first:
                nc.scalar.sem_inc(ots, 2)
                nc.scalar.sem_inc(xnorm, 1)
            with act.Fori(0, ROUNDS) as j:
                if not first:
                    act.wait_ge(vt, j * (NT // 2) + 2)
                    for i in range(NT + LAG):
                        if i < NT:
                            act.wait_ge(otp, j * NT + i + 1)
                            if i >= 2:
                                act.wait_ge(pps, j * NT + i - 1)
                            nc.scalar.copy(OTs[:, i % 2, :, :], psQ[0:CC, i % 2, 0:2 * P].rearrange("p (c t) -> p c t", c=2))\
                                .then_inc(ots, 1)
                        if i >= LAG:
                            t = i - LAG
                            act.wait_ge(xtp, j * NT + t + 1)
                            nc.scalar.copy(XN[:, :, P * t:P * t + P],
                                           psR[0:CC, 2 + t % 2, 0:2 * P].rearrange("p (c t) -> p c t", c=2))\
                                .then_inc(xnorm, 1)
                n = 0
                act.wait_ge(lo, j * NCH + 1)
                if first:
                    act.wait_ge(rlo, j * NR + 4)
                for m in range(NCH + 1):
                    for q in range(PAIR // 512 if m < NCH else 0):
                        act.wait_ge(qps, j * (4 * NCH) + (n + 1))
                        nc.scalar.activation(QF[:, m, 512 * q:512 * q + 512], psQ[:, n % 2, :], ACT.Identity,
                                             bias=BQK[:, m:m + 1], scale=1.0).then_inc(qf, 1)
                        n += 1
                    if m == 1:
                        act.wait_ge(qkst, j * 96 + 16)
                    if m > 0:
                        act.wait_ge(qf, j * (4 * NCH) + (4 * m + 2))
                        nc.scalar.activation(HL[0][:, m - 1, :], QF[:, m - 1, :], ACT.Identity,
                                             scale=SC[:, m - 1:m]).then_inc(hi, 1)
                if first:
                    act.wait_ge(rst, j * 192 + 16)
                    n = 0
                    for g in range(NG):
                        for hw in range(2):
                            for x0 in range(0, HI, RX):
                                act.wait_ge(rps, j * NR + (n + 1))
                                dst, src = rel_views(g, 0, hw, x0, n % 4)
                                for b in range(2):
                                    a = nc.scalar.copy(dst[b], src[b])
                                a.then_inc(rhi, 1)
                                n += 1

        @block.vector
        def _(dve):
            nc.vector.memset(VT[:, :, :, :], 1.0).then_inc(preset, 1)
            nc.vector.sem_inc(vt, 2)
            nc.vector.sem_inc(lo, 1)
            if first:
                nc.vector.sem_inc(xnorm, 1)
                nc.vector.sem_inc(rlo, 4)
            else:
                nc.vector.sem_inc(x2, 4)
            dve.wait_ge(wload, NW)
            dve.wait_ge(preset, 3 if first else 2)
            if first:
                dve.wait_ge(split, 1)
                nc.vector.tensor_tensor(RTS[1][:, :, :, :], RT[:, :, :, :], RTS[0][:, :, :, :], ALU.subtract)\
                    .then_inc(split, 1)

            def link(j, n, ins):
                ins.then_inc(dchain, 1)
                dve.wait_ge(dchain, j * DC + n)

            def channel_moments(j):
                dve.wait_ge(xload, j * 16 + 16)
                for k in range(4):
                    c, b = k % 2, k // 2
                    for h in range(2):
                        t = b * L + 512 * h
                        ins = nc.vector.bn_stats(ST[:, k, h, :], X[:, c, t:t + 512])
                link(j, 1, ins)
                nc.vector.sem_inc(gate, 1)
                for k in range(4):
                    ins = nc.vector.bn_aggr(MV[:, k, :], ST[:, k, :, :].rearrange("p h s -> p (h s)"))
                link(j, 2, ins)

            def group_moments(j):
                dve.wait_ge(gps, j * 2 + 1)
                link(j, 3, nc.vector.tensor_copy(GM[:, :], psR[0:CC, 0, 0:4]))
                link(j, 4, nc.vector.tensor_tensor(D[:, :], MV[:, :, 0], GM[:, :], ALU.subtract))
                link(j, 5, nc.vector.tensor_tensor(D2[:, :], D[:, :], D[:, :], ALU.mult))
                link(j, 6, nc.vector.tensor_tensor(D2[:, :], D2[:, :], MV[:, :, 1], ALU.add))

            def group_variance(j):
                dve.wait_ge(gps, j * 2 + 2)
                link(j, DC, nc.vector.tensor_scalar(VE[:, :], psR[0:CC, 1, 0:4], EPS, None, ALU.add))

            def group_norm(j):
                dve.wait_ge(rsq, j + 1)
                dve.wait_ge(vt, j * (NT // 2) + 2)
                for k in range(4):
                    c, b = k % 2, k // 2
                    nc.vector.tensor_scalar(XN[:, c, b * L:b * L + L], X[:, c, b * L:b * L + L], GM[:, k:k + 1],
                                            RS[:, k:k + 1], ALU.subtract, ALU.mult).then_inc(xnorm, 1)

            def residual_and_norm(j):
                dve.wait_ge(xb, j + 1)
                for q in range(NT // 4 + 1):
                    tiles = range(4 * q, 4 * q + 4)
                    at = j * (3 * NT // 4) + 3 * q
                    if q < NT // 4:
                        for t in tiles:
                            dve.wait_ge(pps, j * NT + (t + 1))
                            nc.vector.tensor_tensor(X[:, t, :], PROJ[t % 4][:, 0:C], X[:, t, :], ALU.add).then_inc(x2, 1)
                        dve.wait_ge(x2, j * NT + (4 * q + 4 + 4))
                        for t in tiles:
                            ins = nc.vector.bn_stats(ST[:, t, :], X[:, t, :])
                        ins.then_inc(st, 1)
                        dve.wait_ge(st, at + 1)
                        nc.vector.sem_inc(gate, 1)
                        for t in tiles:
                            ins = nc.vector.bn_aggr(MV[:, t, :], ST[:, t, :])
                        ins.then_inc(st, 1)
                        dve.wait_ge(st, at + 2)
                        nc.vector.tensor_scalar(VE[:, 4 * q:4 * q + 4], MV[:, 4 * q:4 * q + 4, 1], EPS, None, ALU.add)\
                            .then_inc(st, 1)
                    if q > 0:
                        dve.wait_ge(rsq, j * (NT // 4) + q)
                        for t in range(4 * q - 4, 4 * q):
                            nc.vector.tensor_scalar(XM[:, t, :], X[:, t, :], MV[:, t, 0:1], RS[:, t:t + 1],
                                                    ALU.subtract, ALU.mult).then_inc(xm, 1)

            def low_half(j, m, tokens=slice(0, PAIR)):
                dve.wait_ge(hi, j * NCH + m + 1)
                dve.wait_ge(qkst, j * 96 + 16)
                half = nc.vector.scalar_tensor_tensor(HL[1][:, m, tokens], QF[:, m, tokens], SC[:, m:m + 1],
                                                      HL[0][:, m, tokens], ALU.mult, ALU.subtract)
                if tokens.stop != PAIR:
                    half.then_inc(gate, 1)
                else:
                    half.then_inc(lo, 1)

            def round_of(j, last):
                ahead = first and not last
                if not first:
                    residual_and_norm(j)
                if ahead:
                    channel_moments(j + 1)
                low_half(j, 0)
                if ahead:
                    group_moments(j + 1)
                dve.wait_ge(vst, j * 96 + 16)
                for n in range(NT // 2):
                    if ahead and n == 2:
                        group_variance(j + 1)
                    if first and n == 5:
                        low_half(j, 1)
                    dve.wait_ge(vps, j * (NT // 2) + n + 1)
                    nc.vector.tensor_tensor(
                        VT[:, 2 * n:2 * n + 2, :, 0:HD].rearrange("p t h d -> p (t h) d"),
                        psV[:, n % 2, 0:2 * C].rearrange("p (x d) -> p x d", d=HD),
                        BV2[:, :].rearrange("p (x d) -> p x d", d=HD), ALU.add).then_inc(vt, 1)
                if not first:
                    low_half(j, 1)
                else:
                    n = 0
                    for g in range(NG):
                        for hw in range(2):
                            for x0 in range(0, HI, RX):
                                if n % 4 == 3 and n // 4 < PAIR // 512:
                                    at = 512 * (n // 4)
                                    low_half(j, NCH - 1, slice(at, at + 512))
                                dve.wait_ge(rhi, j * NR + (n + 1))
                                dst, src = rel_views(g, 1, hw, x0, n % 4)
                                high, _ = rel_views(g, 0, hw, x0, n % 4)
                                for b in range(2):
                                    a = nc.vector.tensor_tensor(dst[b], src[b], high[b], ALU.subtract)
                                a.then_inc(rlo, 1)
                                n += 1
                if ahead:
                    group_norm(j + 1)
                if not first:
                    low_half(j, NCH - 1)

            if first:
                channel_moments(0)
                group_moments(0)
                group_variance(0)
                group_norm(0)
            with dve.Fori(0, ROUNDS - 1) as j:
                round_of(j, False)
            round_of(ROUNDS - 1, True)


CAP = T
NTILE = T // P + E_N
LIST = E_N * CAP + NTILE * P
CM = C + 2
EMPTY = 1 << 20


def route(nc, name, X2, ON, WG, BG, X3, SLOTS, TILES):
    NT = PAIR // P
    EPS = 1e-5
    with ExitStack() as ctx:
        def sb(n, shape, dt=F32):
            return ctx.enter_context(nc.sbuf_tensor(f"{name}_{n}", shape, dt))

        def ps(n, shape):
            return ctx.enter_context(nc.psum_tensor(f"{name}_{n}", shape, F32))

        def sem(n):
            return ctx.enter_context(nc.semaphore(f"{name}_{n}"))

        Os = [sb(f"attn{i}", [P, NT, C]) for i in range(2)]
        Xs = [sb(f"x{i}", [P, NT, CM]) for i in range(2)]
        XMs = [sb(f"xm{i}", [P, NT, C]) for i in range(2)]
        XT = sb("xmT", [CC, 2, PAIR])
        ST = sb("stats", [P, NT, 6])
        MV = sb("meanvar", [P, NT, 2])
        VE = sb("variance", [P, NT, 1])
        HALF = sb("half", [P, NT, 1])
        WGs = sb("wg", [CC, 2, E_N])
        BGs = sb("bg", [P, E_N])
        LG = sb("logits", [P, NT, E_N])
        LM = sb("top", [P, NT, 1])
        EQ = sb("isTop", [P, NT, E_N])
        OH = sb("chosen", [P, NT, E_N])
        PRE = [sb(f"chosenUpTo{i}", [P, NT, E_N]) for i in range(2)]
        RUN = sb("chosenBefore", [P, E_N])
        DESC = sb("descending", [P, NT, E_N])
        EB = sb("expertBase", [P, NT, E_N])
        PW = sb("place", [P, NT, E_N])
        PO = sb("placeOf", [P, NT, 1])
        POI = sb("placeOfInt", [P, NT], I32)
        IDF = sb("tokenIds", [P, NT])
        IDI = sb("tokenIdsInt", [P, NT], I32)
        TRI = sb("before", [P, P])
        ONE = sb("ones", [P, P])
        ident = sb("ident", [P, P])
        FILL = sb("empty", [P, LIST // P], I32)
        NTe = sb("tilesOf", [E_N, 1])
        NTi = sb("tilesOfInt", [E_N, 1], I32)
        NTB = sb("tilesOfWide", [E_N, P])
        UPTO = sb("upto", [E_N, E_N])
        END = sb("tileEnds", [P, E_N])
        GE = sb("past", [P, E_N])
        GEE = sb("pastEnds", [P, E_N])
        JP = sb("tileNumber", [P, 1])
        TL = sb("tileList", [P, 2])
        START = sb("tileStart", [P, 1])
        BASE = sb("tileBase", [P, 1])
        TR = sb("tileRows", [2, P], I32)
        psT = ps("psT", [P, 4, 512])
        psL = ps("psL", [P, 512])
        psK = ps("psK", [P, 512])
        psC = ps("psC", [P, 512])

        made = sem("made")
        wload = sem("wload")
        filled = sem("filled")
        load = [sem(f"load{i}") for i in range(2)]
        x3 = sem("x3")
        x3st = [sem(f"x3st{i}") for i in range(2)]
        nm = sem("nm")
        ch = sem("ch")
        xtp = sem("xtp")
        xts = sem("xts")
        lg = sem("lg")
        rk = sem("rk")
        scat = sem("scat")
        idn = sem("idn")
        fin = sem("fin")
        out = sem("out")
        rsq = sem("rsq")
        gate = sem("gate")
        NPRE = NT.bit_length() - 1
        CH = 15 + NPRE
        NM, NM0 = 5, 6
        NMADE = 12

        def rounds(eng, body):
            with eng.Fori(0, ROUNDS // 2 - 1) as i:
                for u in range(2):
                    body(i, u, False)
            for u in range(2):
                body(ROUNDS // 2 - 1, u, u == 1)

        def after(i, u):
            return (i, 1) if u == 0 else (i + 1, 0)

        block = ctx.enter_context(nc.Block())

        @block.sync
        def _(sp):
            for u in range(2):
                nc.sync.sem_inc(x3st[u], 16)
            sp.dma_start(WGs[:], WG.rearrange("(c p) n -> p c n", p=CC)).then_inc(wload, 16)
            sp.dma_start(BGs[:, :], BG.rearrange("(o n) -> o n", o=1).to_broadcast([P, E_N])).then_inc(wload, 16)
            sp.wait_ge(made, NMADE)
            sp.dma_start(SLOTS.rearrange("(p n) o -> p (n o)", p=P), FILL[:, :]).then_inc(filled, 16)
            with sp.Fori(0, ROUNDS // 2) as i:
                for u in range(2):
                    b = i * 2 + u
                    sp.wait_ge(rsq, b + 1)
                    nc.sync.sem_inc(gate, 1)
                    sp.wait_ge(nm, b * NM + 3 + NM0)
                    nc.sync.sem_inc(gate, 1)
                    sp.dma_start(X3[bass.ds(b * PAIR, PAIR), :].rearrange("(t p) c -> p t c", p=P), Xs[u][:, :, :])\
                      .then_inc(x3st[u], 16)
            for u in range(2):
                sp.wait_ge(x3st[u], ROUNDS // 2 * 16 + 16)
            sp.wait_ge(fin, 18)
            sp.dma_start(TILES, TR[:, :]).then_inc(out, 16)
            sp.wait_ge(out, 16)

        @block.gpsimd
        def _(pool):
            nc.gpsimd.sem_inc(idn, 1)
            make_identity(nc, pool, ident, made)
            nc.gpsimd.memset(ONE[:, :], 1.0).then_inc(made, 1)
            pool.wait_ge(made, 3)
            nc.gpsimd.affine_select(out=TRI[:, :], in_=ONE[:, :], compare_op=ALU.is_gt, fill=0.0, base=0,
                                    pattern=[[1, P]], channel_multiplier=-1).then_inc(made, 1)
            nc.gpsimd.affine_select(out=UPTO[:, :], in_=ONE[0:E_N, 0:E_N], compare_op=ALU.is_ge, fill=0.0, base=0,
                                    pattern=[[1, E_N]], channel_multiplier=-1).then_inc(made, 1)
            exact = dict(allow_small_or_imprecise_dtypes=True)
            nc.gpsimd.iota(DESC[:, :, :], [[0, NT], [-1, E_N]], base=E_N, channel_multiplier=0, **exact)\
                .then_inc(made, 1)
            nc.gpsimd.iota(EB[:, :, :], [[0, NT], [CAP, E_N]], base=0, channel_multiplier=0, **exact).then_inc(made, 1)
            nc.gpsimd.iota(IDF[:, :], [[P, NT]], base=0, channel_multiplier=1, **exact).then_inc(made, 1)
            nc.gpsimd.iota(JP[:, :], [[0, 1]], base=0, channel_multiplier=1, **exact).then_inc(made, 1)
            nc.gpsimd.memset(RUN[:, :], 0.0).then_inc(made, 1)
            nc.gpsimd.memset(HALF[:, :, :], -0.5).then_inc(made, 1)
            nc.gpsimd.memset(FILL[:, :], EMPTY).then_inc(made, 1)
            pool.wait_ge(filled, 16)
            pool.wait_ge(made, NMADE)

            def root(i, u):
                pool.wait_ge(nm, (i * 2 + u) * NM + 4 + NM0)
                nc.gpsimd.tensor_tensor(Xs[u][:, :, C + 1:C + 2], VE[:, :, :], HALF[:, :, :], ALU.pow).then_inc(rsq, 1)

            def list_tokens(i, u, last):
                b = i * 2 + u
                if not last:
                    root(*after(i, u))
                pool.wait_ge(ch, b * CH + (CH - 1))
                nc.gpsimd.sem_inc(gate, 1)
                for t in range(NT):
                    pool.indirect_dma_start(SLOTS, bass.IndirectOffsetOnAxis(ap=POI[:, t:t + 1], axis=0),
                                            IDI[:, t:t + 1], None).then_inc(scat, 16)
                pool.wait_ge(scat, b * (16 * NT) + 16 * NT)
                nc.gpsimd.sem_inc(idn, 1)

            root(0, 0)
            rounds(pool, list_tokens)

        @block.tensor
        def _(pe):
            pe.wait_ge(made, NMADE)
            pe.wait_ge(wload, 32)
            def logits_and_ranks(i, u, last):
                b, XM = i * 2 + u, XMs[u]
                pe.wait_ge(nm, b * NM + 5 + NM0)
                for t in range(NT):
                    if t % 2 == 0:
                        pe.wait_ge(xts, b * (NT // 2) + (t // 2 + 1))
                    for c in range(2):
                        at = 2 * P * (t % 2) + P * c
                        mm = nc.tensor.transpose(psT[0:CC, t // 2 % 4, at:at + P], XM[:, t, CC * c:CC * c + CC],
                                                 ident[:, :])
                    if t % 2 == 1:
                        mm.then_inc(xtp, 1)
                pe.wait_ge(xts, b * (NT // 2) + (NT // 2 + 4))
                for t in range(NT):
                    for c in range(2):
                        mm = nc.tensor.matmul(psL[:, E_N * t:E_N * t + E_N], XT[:, c, P * t:P * t + P], WGs[:, c, :],
                                              start=(c == 0), stop=(c == 1))
                mm.then_inc(lg, 1)
                pe.wait_ge(ch, b * CH + 6)
                nc.tensor.matmul(psK[:, 0:NT * E_N], TRI[:, :], OH[:, :, :].rearrange("p t e -> p (t e)"),
                                 start=True, stop=False)
                pe.wait_ge(ch, b * CH + (8 + NPRE))
                nc.tensor.matmul(psK[:, 0:NT * E_N], ONE[:, :], PRE[NPRE % 2][:, :, :].rearrange("p t e -> p (t e)"),
                                 start=False, stop=True).then_inc(rk, 1)

            rounds(pe, logits_and_ranks)
            pe.wait_ge(ch, ROUNDS * CH)
            nc.tensor.matmul(psC[0:E_N, 0:1], RUN[:, :], ONE[:, 0:1], start=True, stop=True).then_inc(fin, 1)
            pe.wait_ge(fin, 5)
            nc.tensor.matmul(psK[:, 0:E_N], NTB[:, :], UPTO[:, :], start=True, stop=True).then_inc(fin, 1)
            pe.wait_ge(fin, 16)
            nc.tensor.transpose(psC[0:2, 0:P], TL[:, :], ident[:, :]).then_inc(fin, 1)

        @block.scalar
        def _(act):
            nc.scalar.sem_inc(xts, 4)

            def load_round(i, u):
                b = i * 2 + u
                act.wait_ge(x3, b + 1)
                act.wait_ge(x3st[u], i * 16 + 16)
                act.wait_ge(nm, b * NM + (NM0 - NM))
                nc.scalar.sem_inc(gate, 1)
                for dst, src in ((Os[u], ON), (Xs[u], X2)):
                    act.dma_start(dst[:, :, 0:C], src[bass.ds(b * PAIR, PAIR), :]
                                  .rearrange("(t p) c -> p t c", p=P)).then_inc(load[u], 16)

            def copies(i, u, last):
                b = i * 2 + u
                if not last:
                    load_round(*after(i, u))
                for n in range(NT // 2):
                    act.wait_ge(xtp, b * (NT // 2) + (n + 1))
                    for t in range(2):
                        a = nc.scalar.copy(XT[:, :, P * (2 * n + t):P * (2 * n + t + 1)],
                                           psT[0:CC, n % 4, 2 * P * t:2 * P * t + 2 * P]
                                           .rearrange("p (c t) -> p c t", c=2))
                    a.then_inc(xts, 1)

            load_round(0, 0)
            rounds(act, copies)

        @block.vector
        def _(dve):
            nc.vector.sem_inc(x3, 2)
            nc.vector.sem_inc(nm, NM0)
            dve.wait_ge(wload, 32)
            dve.wait_ge(made, NMADE)

            def normalise(i, u):
                b = i * 2 + u
                X, O, XM = Xs[u], Os[u], XMs[u]
                n = [0]

                def link(ins):
                    n[0] += 1
                    ins.then_inc(nm, 1)
                    dve.wait_ge(nm, b * NM + (n[0] + NM0))

                dve.wait_ge(load[u], i * 32 + 32)
                nc.vector.tensor_tensor(X[:, :, 0:C], X[:, :, 0:C], O[:, :, :], ALU.add).then_inc(x3, 1)
                dve.wait_ge(x3, b + 3)
                for t in range(NT):
                    ins = nc.vector.bn_stats(ST[:, t, :], X[:, t, 0:C])
                link(ins)
                nc.vector.sem_inc(gate, 1)
                for t in range(NT):
                    ins = nc.vector.bn_aggr(MV[:, t, :], ST[:, t, :])
                link(ins)
                link(nc.vector.tensor_copy(X[:, :, C:C + 1], MV[:, :, 0:1]))
                link(nc.vector.tensor_scalar(VE[:, :, :], MV[:, :, 1:2], EPS, None, ALU.add))
                dve.wait_ge(rsq, b + 1)
                for t in range(NT):
                    ins = nc.vector.tensor_scalar(XM[:, t, :], X[:, t, 0:C], X[:, t, C:C + 1], X[:, t, C + 1:C + 2],
                                                  ALU.subtract, ALU.mult)
                link(ins)
                assert n[0] == NM

            def choose(i, u, last):
                b = i * 2 + u
                n = [0]

                def link(ins):
                    n[0] += 1
                    ins.then_inc(ch, 1)
                    dve.wait_ge(ch, b * CH + n[0])

                if not last:
                    normalise(*after(i, u))
                dve.wait_ge(lg, b + 1)
                link(nc.vector.tensor_tensor(LG[:, :, :], psL[:, 0:NT * E_N].rearrange("p (t e) -> p t e", e=E_N),
                                             BGs[:, :].rearrange("p (o e) -> p o e", o=1).to_broadcast([P, NT, E_N]),
                                             ALU.add))
                link(nc.vector.tensor_reduce(LM[:, :, :], LG[:, :, :], AX.X, ALU.max))
                link(nc.vector.tensor_tensor(EQ[:, :, :], LG[:, :, :], LM[:, :, :].to_broadcast([P, NT, E_N]),
                                             ALU.is_equal))
                link(nc.vector.tensor_tensor(EQ[:, :, :], EQ[:, :, :], DESC[:, :, :], ALU.mult))
                link(nc.vector.tensor_reduce(LM[:, :, :], EQ[:, :, :], AX.X, ALU.max))
                link(nc.vector.tensor_tensor(OH[:, :, :], DESC[:, :, :], LM[:, :, :].to_broadcast([P, NT, E_N]),
                                             ALU.is_equal))
                link(nc.vector.tensor_copy(PRE[0][:, 0, :], RUN[:, :]))
                link(nc.vector.tensor_copy(PRE[0][:, 1:NT, :], OH[:, 0:NT - 1, :]))
                for k in range(NPRE):
                    old, new, d = PRE[k % 2], PRE[(k + 1) % 2], 1 << k
                    nc.vector.tensor_copy(new[:, 0:d, :], old[:, 0:d, :])
                    link(nc.vector.tensor_tensor(new[:, d:NT, :], old[:, d:NT, :], old[:, 0:NT - d, :], ALU.add))
                link(nc.vector.tensor_tensor(RUN[:, :], PRE[NPRE % 2][:, NT - 1, :], OH[:, NT - 1, :], ALU.add))
                dve.wait_ge(rk, b + 1)
                link(nc.vector.tensor_tensor(PW[:, :, :], psK[:, 0:NT * E_N].rearrange("p (t e) -> p t e", e=E_N),
                                             EB[:, :, :], ALU.add))
                link(nc.vector.tensor_tensor(PW[:, :, :], PW[:, :, :], OH[:, :, :], ALU.mult))
                link(nc.vector.tensor_reduce(PO[:, :, :], PW[:, :, :], AX.X, ALU.add))
                dve.wait_ge(idn, b + 1)
                link(nc.vector.tensor_copy(POI[:, :], PO[:, :, 0]))
                link(nc.vector.tensor_copy(IDI[:, :], IDF[:, :]))
                link(nc.vector.tensor_scalar(IDF[:, :], IDF[:, :], float(PAIR), None, ALU.add))
                assert n[0] == CH

            normalise(0, 0)
            rounds(dve, choose)

            def step(at, ins):
                ins.then_inc(fin, 1)
                dve.wait_ge(fin, at)

            dve.wait_ge(fin, 1)
            step(2, nc.vector.tensor_scalar(NTi[:, :], psC[0:E_N, 0:1], float(P - 1), None, ALU.add))
            step(3, nc.vector.tensor_scalar(NTi[:, :], NTi[:, :], 7, None, ALU.arith_shift_right))
            step(4, nc.vector.tensor_copy(NTe[:, :], NTi[:, :]))
            step(5, nc.vector.tensor_copy(NTB[:, :], NTe[:, :].to_broadcast([E_N, P])))
            dve.wait_ge(fin, 6)
            step(7, nc.vector.tensor_copy(END[:, :], psK[:, 0:E_N]))
            step(8, nc.vector.tensor_scalar(GE[:, :], END[:, :], JP[:, :], None, ALU.is_le))
            step(9, nc.vector.tensor_tensor(GEE[:, :], GE[:, :], END[:, :], ALU.mult))
            step(10, nc.vector.tensor_reduce(TL[:, 0:1], GE[:, :], AX.X, ALU.add))
            step(11, nc.vector.tensor_reduce(START[:, :], GEE[:, :], AX.X, ALU.max))
            step(12, nc.vector.tensor_tensor(START[:, :], JP[:, :], START[:, :], ALU.subtract))
            step(13, nc.vector.tensor_scalar(START[:, :], START[:, :], float(P), None, ALU.mult))
            step(14, nc.vector.tensor_scalar(BASE[:, :], TL[:, 0:1], float(CAP), None, ALU.mult))
            step(15, nc.vector.tensor_tensor(TL[:, 1:2], START[:, :], BASE[:, :], ALU.add))
            step(16, nc.vector.tensor_scalar(TL[:, 0:1], TL[:, 0:1], float(E_N - 1), None, ALU.min))
            dve.wait_ge(fin, 17)
            step(18, nc.vector.tensor_copy(TR[:, :], psC[0:2, 0:P]))


def experts(nc, name, X3, SLOTS, TILES, W1, B1, W2, B2, OUT):
    UN = 40
    NB = 8
    LAG = NB - 2
    assert NTILE == 2 * UN and UN % NB == 0
    with ExitStack() as ctx:
        def sb(n, shape, dt=F32):
            return ctx.enter_context(nc.sbuf_tensor(f"{name}_{n}", shape, dt))

        def ps(n, shape):
            return ctx.enter_context(nc.psum_tensor(f"{name}_{n}", shape, F32))

        def sem(n):
            return ctx.enter_context(nc.semaphore(f"{name}_{n}"))

        TLs = sb("tiles", [1, 2, P], I32)
        IXA = sb("slotsAll", [P, NTILE], I32)
        IX = sb("slots", [P, UN], I32)
        WA = sb("w1", [CC + 1, 2, E_N, C])
        WB = sb("w2", [CC + 1, 2, E_N, C])
        XG = sb("x", [P, NB, CM])
        XM = sb("xm", [P, 2, C])
        XT = sb("xmT", [CC + 1, 2, 2, P])
        H = sb("h", [P, 2, C])
        HT = sb("hT", [CC + 1, 2, 2, P])
        Y = sb("y", [P, NB, C])
        ident = sb("ident", [P, P])
        psX = ps("psX", [P, 2, 512])
        psH = ps("psH", [P, 2, 512])
        psG = ps("psG", [P, 2, 512])
        psY = ps("psY", [P, 2, 512])

        tl = sem("tl")
        wl = sem("wl")
        made = sem("made")
        ixa = [sem(f"ixa{i}") for i in range(2)]
        ix = sem("ix")
        got = [sem(f"got{i}") for i in range(NB)]
        put = [sem(f"put{i}") for i in range(NB)]
        free = sem("free")
        xm = sem("xm")
        xtp = sem("xtp")
        xts = sem("xts")
        hp = sem("hp")
        hs = sem("hs")
        htp = sem("htp")
        hts = sem("hts")
        yp = sem("yp")
        ys = sem("ys")
        gate = sem("gate")

        block = ctx.enter_context(nc.Block())

        def load_slots(eng, j0, j1, done):
            with eng.Fori(j0, j1) as j:
                first = eng.value_load(TLs[0:1, 1, bass.ds(j, 1)], min_val=0, max_val=LIST - P)
                with nc.allow_non_contiguous_dma(reason="a slot to each partition"):
                    eng.dma_start(IXA[:, bass.ds(j, 1)], SLOTS[bass.ds(first, P), :]).then_inc(done, 16)

        @block.sync
        def _(sp):
            sp.dma_start(TLs[:, :, :], TILES.rearrange("(o a) b -> o a b", o=1)).then_inc(tl, 16)
            for w, wt, bias in ((WA, W1, B1), (WB, W2, B2)):
                sp.dma_start(w[0:CC], wt.rearrange("(c p) e n -> p c e n", p=CC)).then_inc(wl, 16)
                sp.dma_start(w[CC:CC + 1, 1], bias.rearrange("(o e) n -> o e n", o=1)).then_inc(wl, 16)
            sp.wait_ge(tl, 16)
            nc.sync.sem_inc(ixa[1], 1)
            load_slots(sp, 0, UN // 2, ixa[0])
            load_slots(sp, UN, NTILE, ixa[1])

        @block.gpsimd
        def _(pool):
            make_identity(nc, pool, ident, made)
            pool.wait_ge(made, 2)
            nc.gpsimd.memset(XT[CC:CC + 1], 1.0).then_inc(made, 1)
            pool.wait_ge(made, 3)
            nc.gpsimd.memset(HT[CC:CC + 1], 1.0).then_inc(made, 1)
            pool.wait_ge(made, 4)
            nc.gpsimd.memset(XG[:, :, :], 0.0).then_inc(made, 1)
            pool.wait_ge(made, 5)
            pool.wait_ge(ixa[0], 16 * UN)

            def put_back(i, k):
                q = k % NB
                pool.wait_ge(ys, i * UN + (k + 1 + 2))
                nc.gpsimd.sem_inc(gate, 1)
                pool.indirect_dma_start(OUT, bass.IndirectOffsetOnAxis(ap=IX[:, k:k + 1], axis=0), Y[:, q, :], None,
                                        bounds_check=T - 1, oob_is_err=False).then_inc(put[q], 16)

            with pool.Fori(0, NTILE // UN) as i:
                pool.wait_ge(ixa[1], i * (16 * UN) + 1)
                nc.gpsimd.sem_inc(gate, 1)
                nc.gpsimd.tensor_copy(IX[:, :], IXA[:, bass.ds(i * UN, UN)]).then_inc(ix, 1)
                pool.wait_ge(ix, i + 1)
                nc.gpsimd.sem_inc(gate, 1)
                for k in range(UN):
                    q = k % NB
                    if k >= NB:
                        pool.wait_ge(put[q], i * (16 * UN // NB) + 16 * (k // NB))
                    nc.gpsimd.sem_inc(free, 1)
                    pool.indirect_dma_start(XG[:, q, :], None, X3, bass.IndirectOffsetOnAxis(ap=IX[:, k:k + 1], axis=0),
                                            bounds_check=T - 1, oob_is_err=False).then_inc(got[q], 16)
                    if k >= LAG:
                        put_back(i, k - LAG)
                for k in range(UN - LAG, UN):
                    put_back(i, k)
                for q in range(NB):
                    pool.wait_ge(put[q], i * (16 * UN // NB) + 16 * (UN // NB))
                nc.gpsimd.sem_inc(gate, 1)

        @block.tensor
        def _(pe):
            pe.wait_ge(made, 5)
            pe.wait_ge(tl, 16)
            pe.wait_ge(wl, 64)

            def turn(dst, src, done):
                for c in range(2):
                    mm = nc.tensor.transpose(dst[0:CC, P * c:P * c + P], src[:, CC * c:CC * c + CC], ident[:, :])
                mm.then_inc(done, 1)

            def layer(dst, xT, w, e, done):
                for c in range(2):
                    k = CC + c
                    mm = nc.tensor.matmul(dst[:, 0:C], xT[0:k, c, :], w[0:k, c, bass.ds(e, 1), :]
                                          .rearrange("p o n -> p (o n)"), start=(c == 0), stop=(c == 1))
                mm.then_inc(done, 1)

            with pe.Fori(0, NTILE // UN) as i:
                ex = [None] * UN
                for k in range(UN + 3):
                    n = i * UN
                    if k < UN:
                        pe.wait_ge(xm, n + (k + 1))
                        pe.wait_ge(xts, n + (k + 1))
                        turn(psX[:, k % 2, :], XM[:, k % 2, :], xtp)
                    if 1 <= k <= UN:
                        m = k - 1
                        ex[m] = pe.value_load(TLs[0:1, 0, bass.ds(n + m, 1)], min_val=0, max_val=E_N - 1)
                        pe.wait_ge(xts, n + (m + 1 + 2))
                        pe.wait_ge(hs, n + (m + 1))
                        layer(psH[:, m % 2, :], XT[:, m % 2], WA, ex[m], hp)
                    if 2 <= k <= UN + 1:
                        m = k - 2
                        pe.wait_ge(hs, n + (m + 1 + 2))
                        pe.wait_ge(hts, n + (m + 1))
                        turn(psG[:, m % 2, :], H[:, m % 2, :], htp)
                    if 3 <= k:
                        m = k - 3
                        pe.wait_ge(hts, n + (m + 1 + 2))
                        pe.wait_ge(ys, n + (m + 1))
                        layer(psY[:, m % 2, :], HT[:, m % 2], WB, ex[m], yp)

        @block.scalar
        def _(act):
            nc.scalar.sem_inc(xts, 2)
            nc.scalar.sem_inc(hs, 2)
            nc.scalar.sem_inc(hts, 2)
            act.wait_ge(tl, 16)
            load_slots(act, UN // 2, UN, ixa[0])
            act.wait_ge(made, 5)

            def to_sbuf(dst, src, done):
                nc.scalar.copy(dst[0:CC], src[0:CC, 0:2 * P].rearrange("p (c t) -> p c t", c=2)).then_inc(done, 1)

            with act.Fori(0, NTILE // UN) as i:
                n = i * UN
                for k in range(UN + 2):
                    if k < UN:
                        act.wait_ge(xtp, n + (k + 1 + 2))
                        act.wait_ge(hp, n + (k + 1))
                        to_sbuf(XT[:, k % 2], psX[:, k % 2, :], xts)
                    if 1 <= k <= UN:
                        m = k - 1
                        act.wait_ge(hp, n + (m + 1 + 2))
                        nc.scalar.activation(H[:, m % 2, :], psH[:, m % 2, 0:C], ACT.Gelu).then_inc(hs, 1)
                    if 2 <= k:
                        m = k - 2
                        act.wait_ge(htp, n + (m + 1))
                        act.wait_ge(yp, n + (m + 1))
                        to_sbuf(HT[:, m % 2], psG[:, m % 2, :], hts)

        @block.vector
        def _(dve):
            nc.vector.sem_inc(xtp, 2)
            nc.vector.sem_inc(hp, 2)
            nc.vector.sem_inc(yp, 2)
            nc.vector.sem_inc(ys, 2)
            with dve.Fori(0, NTILE // UN) as i:
                n = i * UN
                for k in range(UN + 4):
                    if k < UN:
                        q, p = k % NB, k % 2
                        dve.wait_ge(got[q], i * (16 * UN // NB) + 16 * (k // NB + 1))
                        dve.wait_ge(xtp, n + (k + 1))
                        nc.vector.tensor_scalar(XM[:, p, :], XG[:, q, 0:C], XG[:, q, C:C + 1], XG[:, q, C + 1:CM],
                                                ALU.subtract, ALU.mult).then_inc(xm, 1)
                    if k >= 4:
                        m = k - 4
                        dve.wait_ge(yp, n + (m + 1 + 2))
                        dve.wait_ge(free, n + (m + 1))
                        nc.vector.tensor_tensor(Y[:, m % NB, :], psY[:, m % 2, 0:C], XG[:, m % NB, 0:C], ALU.add)\
                            .then_inc(ys, 1)


def hybrid_block(nc, a, out):
    def dram(n, shape, dt=F32):
        return nc.dram_tensor(n, shape, dt, kind=DRAM_KIND).ap()

    QK1 = dram("qk1", (B, 2, 2 * C, L), F16)
    RL1 = dram("rel1", (STEPS, 2, 2, P, L), F16)
    VN1 = dram("v1", (STEPS, P, KT, GH, VW))
    O1 = dram("attn1", (T, C))
    X2 = dram("x2", (T, C))
    QK2 = dram("qk2", (B, 2, 2 * C, L), F16)
    VN2 = dram("v2", (STEPS, P, KT, GH, VW))
    O2 = dram("attn2", (T, C))
    X3 = dram("x3", (T, CM))
    SLOTS = dram("slots", (LIST, 1), I32)
    TILES = dram("tiles", (2, P), I32)
    const = {"group": a["group"], "sc": a["sc1"]}
    project(nc, "p1", True, a["xT"], {"wqk": a["c_wqk"], "bqk": a["c_bqk"], "wv": a["c_wv"], "bv": a["c_bv"],
                                      "relT": a["relT"]}, const, QK1, VN1, RL=RL1)
    attention(nc, "a1", True, 1.0, QK1, RL1, VN1, O1, a["onehot"])
    const = {"group": a["group"], "sc": a["sc2"]}
    project(nc, "p2", False, a["x"], {"wqk": a["a_wqk"], "bqk": a["a_bqk"], "wv": a["a_wv"], "bv": a["a_bv"],
                                      "proj_w": a["proj_w"], "proj_b": a["proj_b"]}, const, QK2, VN2, ON=O1, X2=X2)
    attention(nc, "a2", False, 1.0 / float(np.sqrt(C)), QK2, None, VN2, O2, a["onehot"])
    route(nc, "r", X2, O2, a["wg"], a["bg"], X3, SLOTS, TILES)
    experts(nc, "e", X3, SLOTS, TILES, a["w1"], a["b1"], a["w2"], a["b2"], out)


DRAM_KIND = "Internal"


def constants():
    t = np.arange(L)
    onehot = np.zeros((REL + 2, L), np.float16)
    onehot[t // WI, t] = 1
    onehot[HI + t % WI, t] = 1
    onehot[REL] = MAXSCALE
    c = np.arange(CC)
    n = C // GROUPS
    group = ((c[:, None] // n == c[None, :] // n) / n).astype(np.float32)
    rows = np.arange(NCH)[None, :] * P + np.arange(P)[:, None]
    sc1 = np.where(rows < C, 1.0, HD ** -0.5).astype(np.float32)
    return {"onehot": onehot, "group": group, "sc1": sc1, "sc2": np.ones((P, NCH), np.float32)}


def kernel(**inputs):
    import concourse.bacc as _bacc
    from concourse.bass_utils import run_bass_kernel_spmd as _run

    i = {k: np.asarray(v) for k, v in inputs.items()}
    x = i["x"].reshape(T, C)
    qkv_w, qkv_b = i["L0_conv_qkv_w"], i["L0_conv_qkv_b"]
    given = {
        "x": x, "xT": x.T,
        "c_wqk": qkv_w[:, :2 * C], "c_bqk": qkv_b[:2 * C], "c_wv": qkv_w[:, 2 * C:], "c_bv": qkv_b[2 * C:],
        "relT": np.stack([i["L0_conv_rel_pos_h"][::-1].T, i["L0_conv_rel_pos_w"][::-1].T]),
        "proj_w": i["L0_conv_proj_w"], "proj_b": i["L0_conv_proj_b"],
        "a_wqk": np.concatenate([i["L1_attn_Wq"], i["L1_attn_Wk"]], 1),
        "a_bqk": np.concatenate([i["L1_attn_bq"], i["L1_attn_bk"]]),
        "a_wv": i["L1_attn_Wv"], "a_bv": i["L1_attn_bv"],
        "wg": i["L1_ffn_Wg"].T, "bg": i["L1_ffn_bg"],
        "w1": i["L1_ffn_W1"].transpose(2, 0, 1), "b1": i["L1_ffn_b1"],
        "w2": i["L1_ffn_W2"].transpose(2, 0, 1), "b2": i["L1_ffn_b2"],
        **constants(),
    }
    nc = _bacc.Bacc("TRN2", target_bir_lowering=False, num_devices=1)
    arrays, aps = {}, {}
    for name, a in given.items():
        a = np.ascontiguousarray(a)
        arrays[f"in_{name}"] = a
        aps[name] = nc.dram_tensor(f"in_{name}", a.shape, mybir.dt.from_np(a.dtype), kind="ExternalInput").ap()
    out = nc.dram_tensor("out_0", (T, C), F32, kind="ExternalOutput").ap()
    hybrid_block(nc, aps, out)
    r = _run(nc, [arrays], core_ids=[0])
    return r.results[0]["out_0"].reshape(B, HI, WI, C)
```
